# Optimizing a Trainium2 kernel written in Bass

```python
import numpy as np
import jax
import jax.numpy as jnp

def _softmax(x, axis=-1):
    return jax.nn.softmax(x, axis=axis)

def _gelu(x):
    return jax.nn.gelu(x, approximate=True)

def _silu(x):
    return jax.nn.silu(x)

def _sigmoid(x):
    return jax.nn.sigmoid(x)

def _layernorm(x, axis=-1, eps=1e-05):
    m = jnp.mean(x, axis=axis, keepdims=True)
    v = jnp.var(x, axis=axis, keepdims=True)
    return (x - m) / jnp.sqrt(v + eps)

def _scatter_add(tgt, idx, src, axis=0):
    return tgt.at[idx].add(src)

def _segment_sum(src, seg, n):
    return jax.ops.segment_sum(src, seg, n)
kernel_name = 'mk_sandwich_d1_jaxref_r4_d9494c'

def setup_inputs(seed: int=0):
    np.random.seed(seed)
    _w = jnp.asarray

    def _L0_attn_setup():
        import jax, jax.numpy as jnp
        import numpy as np
        B, S, D = (8, 512, 256)
        EPS = 1e-07

        def _loc_weights(steps):
            idx = jnp.arange(steps)
            location = jnp.abs(idx[None, :] - idx[:, None]).astype(jnp.float32)
            lw = 1.0 / (location + EPS) * (location != 0).astype(jnp.float32)
            return lw
        key = jax.random.key(seed)
        kx, kw = jax.random.split(key)
        x = jax.random.normal(kx, (B, S, D), dtype=jnp.float32)
        limit = float(np.sqrt(6.0 / (D + D)))
        W = jax.random.uniform(kw, (D, D), dtype=jnp.float32, minval=-limit, maxval=limit)
        b = jnp.zeros((D,), dtype=jnp.float32)
        return {'x': x, 'W': W, 'b': b}
    _L0_attn_in = _L0_attn_setup()

    def _L0_ffn_setup():
        import jax, jax.numpy as jnp
        import numpy as np
        B, T, H = (8, 512, 256)
        F = 1024
        E = 8
        TOP_K = 2
        key = jax.random.key(seed)
        ks = jax.random.split(key, 6)
        s_h = 1.0 / np.sqrt(H)
        s_f = 1.0 / np.sqrt(F)
        return {'hidden_states': jax.random.normal(ks[0], (B, T, H), dtype=jnp.float32), 'gate_w': jax.random.uniform(ks[1], (H, E), minval=-s_h, maxval=s_h, dtype=jnp.float32), 'w1': jax.random.uniform(ks[2], (E, H, F), minval=-s_h, maxval=s_h, dtype=jnp.float32), 'b1': jax.random.uniform(ks[3], (E, F), minval=-s_h, maxval=s_h, dtype=jnp.float32), 'w2': jax.random.uniform(ks[4], (E, F, H), minval=-s_f, maxval=s_f, dtype=jnp.float32), 'b2': jax.random.uniform(ks[5], (E, H), minval=-s_f, maxval=s_f, dtype=jnp.float32)}
    _L0_ffn_in = _L0_ffn_setup()
    _d = {'L0_attn_x': _L0_attn_in['x'], 'L0_attn_W': _L0_attn_in['W'], 'L0_attn_b': _L0_attn_in['b'], 'L0_ffn_gate_w': _L0_ffn_in['gate_w'], 'L0_ffn_w1': _L0_ffn_in['w1'], 'L0_ffn_b1': _L0_ffn_in['b1'], 'L0_ffn_w2': _L0_ffn_in['w2'], 'L0_ffn_b2': _L0_ffn_in['b2']}
    _x0 = _d['L0_attn_x']
    _d['L0_attn_x'] = jax.random.normal(jax.random.fold_in(jax.random.key(seed), 1), (1, 4096, 256), dtype=_x0.dtype)
    del _x0
    return _d

def reference(L0_attn_x, L0_attn_W, L0_attn_b, L0_ffn_gate_w, L0_ffn_w1, L0_ffn_b1, L0_ffn_w2, L0_ffn_b2):

    def _L0_attn_ref(x, W, b):
        import jax, jax.numpy as jnp
        import numpy as np
        B, S, D = (8, 512, 256)
        EPS = 1e-07

        def _loc_weights(steps):
            idx = jnp.arange(steps)
            location = jnp.abs(idx[None, :] - idx[:, None]).astype(jnp.float32)
            lw = 1.0 / (location + EPS) * (location != 0).astype(jnp.float32)
            return lw
        steps = x.shape[1]
        x_tran = jnp.matmul(x, W) + b
        weights = jnp.einsum('bsd,btd->bst', x_tran, x)
        lw = _loc_weights(steps)
        weights = jnp.exp(jnp.tanh(weights * lw))
        off_diag = 1.0 - jnp.eye(steps, dtype=weights.dtype)
        weights = weights * off_diag
        weights = weights / (jnp.sum(weights, axis=-1, keepdims=True) + EPS)
        return jnp.matmul(weights, x)

    def _L0_ffn_ref(hidden_states, gate_w, w1, b1, w2, b2):
        import jax, jax.numpy as jnp
        import numpy as np
        B, T, H = (8, 512, 256)
        F = 1024
        E = 8
        TOP_K = 2
        b, t, h = hidden_states.shape
        seq_rep = hidden_states.mean(axis=1)
        router_logits = seq_rep @ gate_w
        probs = jax.nn.softmax(router_logits.astype(jnp.float32), axis=-1)
        top_w, top_i = jax.lax.top_k(probs, TOP_K)
        top_w = top_w / top_w.sum(axis=-1, keepdims=True)
        top_w = top_w.astype(hidden_states.dtype)
        combine = jnp.zeros((b, E), dtype=hidden_states.dtype)
        combine = combine.at[jnp.arange(b)[:, None], top_i].set(top_w)
        out = jnp.zeros_like(hidden_states)
        for e in range(E):
            hmid = jax.nn.gelu(jnp.einsum('bth,hf->btf', hidden_states, w1[e]) + b1[e], approximate=False)
            y = jnp.einsum('btf,fh->bth', hmid, w2[e]) + b2[e]
            out = out + combine[:, e][:, None, None] * y
        return out
    x = L0_attn_x
    x = x + _layernorm(_L0_attn_ref(_layernorm(x, axis=-1), L0_attn_W, L0_attn_b), axis=-1)
    x = x + _layernorm(_L0_ffn_ref(_layernorm(x, axis=-1), L0_ffn_gate_w, L0_ffn_w1, L0_ffn_b1, L0_ffn_w2, L0_ffn_b2), axis=-1)
    return x

_drawn_inputs = setup_inputs


def setup_inputs(seed=0):
    import zlib

    import numpy as np

    out = dict(_drawn_inputs(seed))
    spreads = {'L0_attn_b': (0.0, 0.474)}
    factors = {}
    for name, (base, spread) in spreads.items():
        noise = np.random.default_rng([zlib.crc32(name.encode()), seed]).standard_normal(out[name].shape)
        drawn = base * np.exp(spread * noise) if base else spread * noise
        out[name] = jnp.asarray(drawn.astype(out[name].dtype))
    for name, factor in factors.items():
        out[name] = (out[name] * factor).astype(out[name].dtype)
    return out
```

```python
from contextlib import ExitStack

import concourse.bass as bass
from concourse import mybir

ALU = mybir.AluOpType
ACT = mybir.ActivationFunctionType
AX_X = mybir.AxisListType.X
F32 = mybir.dt.float32
F16 = mybir.dt.float16
I32 = mybir.dt.int32

P = 128
EPS_LN = 1e-5
EPS_W = 1e-7
WSCALE = 16.0
TOP = 2


def program(nc, x_d, W_d, b_d, gate_d, w1_d, b1_d, w2_d, b2_d, out_d):
    _, S, D = x_d.shape
    E, _, F = w1_d.shape
    KD = D // P
    NT = S // P
    IB = 512
    TB = IB // P
    NB = S // IB
    NP = NT // 2
    BLK = KD * IB
    VW = 2 * D + 2
    VLO = D + 2
    LWOFF = S - P
    LWW = LWOFF + S
    LWC = LWW // 4
    FT = F // P
    FP = FT // 2
    NQ = TOP * FP
    FC = 2 * P
    LWA = max(LWW, NQ * (KD * FC + 2 * D))
    EC = 10 + 2 * TB

    with ExitStack() as ctx:
        def sb(name, shape, dt=F32):
            return ctx.enter_context(nc.sbuf_tensor(name, shape, dt))

        def sem(name):
            return ctx.enter_context(nc.semaphore(name))

        xres = sb("xres", [P, NT, D])
        lw = sb("lw", [P, LWA])
        vmat = sb("vmat", [P, NT * VW], F16)
        xnTh = sb("xnTh", [P, NB * BLK], F16)
        xnTl = sb("xnTl", [P, NB * BLK], F16)
        xtTh = sb("xtTh", [P, NB * BLK], F16)
        xtTl = sb("xtTl", [P, NB * BLK], F16)
        zbuf = sb("zbuf", [P, 2, 2 * IB])
        ebuf = sb("ebuf", [P, 2, 2 * IB])
        ph = sb("ph", [P, 2, 2 * IB], F16)
        pl = sb("pl", [P, 2, 2 * IB], F16)
        accs = sb("accs", [P, TB, D + 1])
        hsum = sb("hsum", [P, D])
        bprod = sb("bprod", [P, TOP, FT, E])
        xn_f = sb("xn_f", [P, 2, TB, D])
        Wh = sb("Wh", [P, KD, D], F16)
        Wl = sb("Wl", [P, KD, D], F16)
        bcol = sb("bcol", [P, KD])
        gate = sb("gate", [P, KD, E])
        b1rows = sb("b1rows", [E * FT, P])
        b1cols = sb("b1cols", [P, E * FT])
        b1sel = sb("b1sel", [P, TOP * FT])
        ident = sb("ident", [P, P], F16)
        identf = sb("identf", [P, P])
        ones = sb("ones", [P, P])
        tcol = sb("tcol", [P, 1])
        half = sb("half", [P, 2 * TB])
        stats = sb("stats", [P, 2, TB, 6])
        mv = sb("mv", [P, 2, TB, 2])
        rstd = sb("rstd", [P, 2, TB])
        rden = sb("rden", [P, TB])
        den = sb("den", [P, TB])
        kfac = sb("kfac", [P, TB])
        vsc = sb("vsc", [P, 2, TB])
        htot = sb("htot", [P, D])
        vtmp = sb("vtmp", [P, 2, TB])
        meanT = sb("meanT", [P, KD])
        meanB = sb("meanB", [P, KD, P])
        rt = sb("rt", [P, 12, E])
        rc = sb("rc", [P, 16])
        rev = sb("rev", [P, E])
        eidx = sb("eidx", [P, TOP], I32)
        comb = sb("comb", [P, E])
        b2c = sb("b2c", [P, D])

        Wf = zbuf[:, 0, 0:KD * D].rearrange("p (k n) -> p k n", k=KD)
        xtf = ebuf[:, 0, :].rearrange("p (k c) -> p k c", k=KD)
        b2all = xn_f[:, :, :, :].rearrange("p u t d -> p (u t) d")
        w1f = lw[:, 0:NQ * KD * FC].rearrange("p (q k f) -> p q k f", q=NQ, k=KD)
        w2f = lw[:, NQ * KD * FC:NQ * KD * FC + NQ * 2 * D].rearrange("p (q s d) -> p q s d", q=NQ, s=2)
        n_w = NQ * KD * FC

        def wview(n):
            return vmat[:, n * n_w:(n + 1) * n_w].rearrange("p (q k f) -> p q k f", q=NQ, k=2)
        w1h, w1l, w2h, w2l = (wview(n) for n in range(4))

        sc = ctx.enter_context(nc.psum_tensor("sc", [P, 2, 2, IB], F32))
        acc = ctx.enter_context(nc.psum_tensor("acc", [P, TB, 512], F32))

        x_in = [sem(f"x_in{g}") for g in range(NB)]
        w_in = sem("w_in")
        small_in = sem("small_in")
        b2_in = sem("b2_in")
        labs_ok = sem("labs_ok")
        leps_ok = sem("leps_ok")
        lrcp_ok = sem("lrcp_ok")
        lw_ok = sem("lw_ok")
        consts = sem("consts")
        ident_ok = sem("ident_ok")
        iota_ok = sem("iota_ok")
        ones_col = sem("ones_col")
        st_ok = sem("st_ok")
        mv_ok = sem("mv_ok")
        xtf_ok = sem("xtf_ok")
        ec = sem("ec")
        x1_kept = sem("x1_kept")
        hs_ok = sem("hs_ok")
        rchain = sem("rchain")
        fc = sem("fc")
        var_ok = sem("var_ok")
        rstd_ok = sem("rstd_ok")
        xn_ok = sem("xn_ok")
        vh_ok = sem("vh_ok")
        vl_ok = sem("vl_ok")
        w_hi = sem("w_hi")
        w_lo = sem("w_lo")
        tp_ok = sem("tp_ok")
        tp_hi = sem("tp_hi")
        tp_lo = sem("tp_lo")
        xt_ok = sem("xt_ok")
        xt_hi = sem("xt_hi")
        xt_lo = sem("xt_lo")
        scores_ok = sem("scores_ok")
        z_ok = sem("z_ok")
        tanh_ok = sem("tanh_ok")
        exp_ok = sem("exp_ok")
        phi_ok = sem("phi_ok")
        p_ok = sem("p_ok")
        pv_ok = sem("pv_ok")
        acc_out = sem("acc_out")
        epi_ok = sem("epi_ok")
        b1t_ok = sem("b1t_ok")
        b1c_ok = sem("b1c_ok")
        hmean_ok = sem("hmean_ok")
        meanT_ok = sem("meanT_ok")
        logit_ok = sem("logit_ok")
        lmax_ok = sem("lmax_ok")
        lexp_ok = sem("lexp_ok")
        route_ok = sem("route_ok")
        w1_in = [sem(f"w1_in{q}") for q in range(NQ)]
        w2_in = [sem(f"w2_in{q}") for q in range(NQ)]
        b1sel_ok = sem("b1sel_ok")
        w1_hi = sem("w1_hi")
        w1_lo = sem("w1_lo")
        w2_sc = sem("w2_sc")
        w2_hi = sem("w2_hi")
        w2_lo = sem("w2_lo")
        ht_ok = sem("ht_ok")
        ht_hi = sem("ht_hi")
        ht_lo = sem("ht_lo")
        up_ok = sem("up_ok")
        gelu_ok = sem("gelu_ok")
        ghi_ok = sem("ghi_ok")
        g_ok = sem("g_ok")
        down_ok = sem("down_ok")
        y_out = sem("y_out")
        fin_ok = sem("fin_ok")
        store_ok = sem("store_ok")

        def vtile(t, lo, n):
            base = t * VW + lo
            return vmat[:, base:base + n] if isinstance(t, int) else vmat[:, bass.ds(base, n)]

        def vblock(g, lo, n):
            return bass.AP(vmat, g * TB * VW + lo, [[NT * VW, P], [VW, TB], [1, n]])

        def tr(buf, g, k, c, n):
            return buf[:, bass.ds(g * BLK + k * IB + c, n)]

        def lwpair(b, jp):
            return bass.AP(lw, LWOFF + IB * b - 2 * P * jp - P, [[LWA, P], [P, 2], [1, IB]])

        acc16 = acc[:, :, :].bitcast(F16)
        sc16 = sc[:, :, :, :].bitcast(F16)

        block = ctx.enter_context(nc.Block())

        @block.sync
        def _(sp):
            xv = x_d[0].rearrange("(g t p) d -> g p t d", t=TB, p=P)
            for g in range(NB):
                sp.dma_start(xres[:, TB * g:TB * g + TB, :], xv[g]).then_inc(x_in[g], 16)
                if g == 0:
                    sp.dma_start(Wf[:, :, :], W_d.rearrange("(k p) n -> p k n", p=P)).then_inc(w_in, 16)

            sp.wait_ge(route_ok, TOP)
            for e in range(TOP):
                ex = sp.value_load(eidx[0:1, e:e + 1], min_val=0, max_val=E - 1)
                for f in range(FP):
                    q = e * FP + f
                    sp.dma_start(w1f[:, q], w1_d[bass.ds(ex, 1), :, f * FC:(f + 1) * FC]
                                 .rearrange("a (k p) f -> p (a k) f", p=P)).then_inc(w1_in[q], 16)
                    sp.dma_start(w2f[:, q], w2_d[bass.ds(ex, 1), f * FC:(f + 1) * FC, :]
                                 .rearrange("a (s p) d -> p (a s) d", p=P)).then_inc(w2_in[q], 16)
            ov = out_d[0].rearrange("(g t p) d -> g p t d", t=TB, p=P)
            for g in range(NB):
                sp.wait_ge(fin_ok, g + 1)
                sp.dma_start(ov[g], xres[:, TB * g:TB * g + TB, :]).then_inc(store_ok, 16)
            sp.wait_ge(store_ok, 16 * NB)

        @block.gpsimd
        def _(pool):
            pool.memset(half[:, :], -0.5).then_inc(consts, 1)
            pool.memset(ident[:, :], 0.0).then_inc(consts, 1)
            pool.memset(identf[:, :], 0.0).then_inc(consts, 1)
            pool.wait_ge(consts, 3)
            for m in (ident, identf):
                pool.affine_select(out=m[:, :], in_=m[:, :], compare_op=ALU.not_equal, fill=1.0, base=0,
                                   pattern=[[-1, P]], channel_multiplier=1).then_inc(ident_ok, 1)
            pool.memset(vmat[:, :].rearrange("p (t w) -> p t w", w=VW)[:, :, D:D + 2], 1.0).then_inc(ones_col, 1)
            pool.memset(ones[:, :], 1.0).then_inc(consts, 1)
            pool.memset(tcol[:, :], 1.0 / S).then_inc(consts, 1)
            pool.memset(hsum[:, :], 0.0).then_inc(consts, 1)
            pool.iota(rev[:, :], [[-1, E]], base=E, channel_multiplier=0,
                      allow_small_or_imprecise_dtypes=True).then_inc(consts, 1)
            pool.dma_start(gate[:, :, :], gate_d.rearrange("(k p) e -> p k e", p=P)).then_inc(small_in, 16)
            pool.dma_start(bcol[:, :], b_d.rearrange("(k p) -> p k", p=P), allow_slow_non_contiguous=True).then_inc(small_in, 16)
            pool.dma_start(b1rows[:, :], b1_d.rearrange("e (t p) -> (e t) p", p=P)).then_inc(small_in, 16)

            def power(n, u):
                pool.wait_ge(var_ok, n + 1)
                pool.tensor_tensor(rstd[:, u, :], vtmp[:, u, :], half[:, 0:TB], ALU.pow).then_inc(rstd_ok, 1)

            power(0, 0)
            for g in range(NB):
                if g < 4:
                    pool.iota(lw[:, g * LWC:(g + 1) * LWC], [[1, LWC]], base=g * LWC - LWOFF,
                              channel_multiplier=-1, allow_small_or_imprecise_dtypes=True).then_inc(iota_ok, 1)
                if g + 1 < NB:
                    power(g + 1, (g + 1) % 2)
                if g >= 1 and g < 5:
                    pool.wait_ge(labs_ok, g)
                    pool.tensor_scalar(lw[:, (g - 1) * LWC:g * LWC], lw[:, (g - 1) * LWC:g * LWC], EPS_W, None,
                                       ALU.add).then_inc(leps_ok, 1)
                pool.wait_ge(vh_ok, g + 1)
                pool.tensor_tensor(vblock(g, VLO, D), xn_f[:, g % 2], vblock(g, 0, D),
                                   ALU.subtract).then_inc(vl_ok, 1)
            pool.wait_ge(lrcp_ok, 4)
            pool.affine_select(out=lw[:, LWOFF:LWOFF + P], in_=lw[:, LWOFF:LWOFF + P], compare_op=ALU.not_equal,
                               fill=0.0, base=0, pattern=[[1, P]], channel_multiplier=-1).then_inc(lw_ok, 1)
            pool.wait_ge(vh_ok, NB)
            pool.wait_ge(vl_ok, NB)
            pool.dma_start(b2all, bass.AP(b2_d.tensor, 0, [[0, P], [D, E], [1, D]])).then_inc(b2_in, 16)
            with pool.Fori(0, NB) as b:
                for u in range(2):
                    power(NB + 2 * b + u, u)
            with pool.Fori(0, NB) as b:
                power(3 * NB + b, 0)

        @block.tensor
        def _(pe):
            pe.wait_ge(ident_ok, 2)
            for g in range(NB):
                for h in range(2):
                    n = 2 * g + h
                    if h == 0:
                        pe.wait_ge(vh_ok, g + 1)
                        pe.wait_ge(vl_ok, g + 1)
                    if n >= 2:
                        pe.wait_ge(tp_hi, n - 1)
                        pe.wait_ge(tp_lo, n - 1)
                    for part, lo in enumerate((0, VLO)):
                        for k in range(KD):
                            for s in range(2):
                                at = (part * KD + k) * 2 * P + s * P
                                mm = pe.transpose(acc16[:, n % 2, at:at + P],
                                                  vtile(2 * n + s, lo + k * P, P), ident[:, :])
                    mm.then_inc(tp_ok, 1)
                if g == 0:
                    pe.wait_ge(w_hi, 1)
                    pe.wait_ge(w_lo, 1)
                pe.wait_ge(tp_hi, 2 * g + 2)
                pe.wait_ge(tp_lo, 2 * g + 2)
                if g >= 2:
                    pe.wait_ge(xt_lo, KD * (g - 1))
                for m in range(KD):
                    for i, (wp, xp) in enumerate(((Wh, xnTh), (Wl, xnTh), (Wh, xnTl))):
                        for k in range(KD):
                            mm = pe.matmul(sc[:, g % 2, m, :], wp[:, k, m * P:(m + 1) * P],
                                           tr(xp, g, k, 0, IB),
                                           start=(i == 0 and k == 0), stop=(i == 2 and k == KD - 1))
                mm.then_inc(xt_ok, 1)
            pe.wait_ge(small_in, 48)
            pe.transpose(acc[:, 2, 0:E * FT], b1rows[:, :], identf[0:E * FT, 0:E * FT]).then_inc(b1t_ok, 1)

            def scores(b, h, u, first=False):
                if not first:
                    pe.wait_ge(z_ok, b * NP + 2 * h + u - 1)
                for s in range(2):
                    for i, (jm, im) in enumerate(((xnTh, xtTh), (xnTl, xtTh), (xnTh, xtTl))):
                        for k in range(KD):
                            mm = pe.matmul(sc[:, u, s, :], tr(jm, h, k, (2 * u + 1 - s) * P, P), tr(im, b, k, 0, IB),
                                           start=(i == 0 and k == 0), stop=(i == 2 and k == KD - 1))
                mm.then_inc(scores_ok, 1)

            def pv(b, jp, u, start=False, stop=False, fresh=False):
                pe.wait_ge(p_ok, b * NP + jp + 1)
                for t in range(TB):
                    if start and not fresh:
                        pe.wait_ge(acc_out, TB * (b - 1) + t + 1)
                    for s in range(2):
                        c = s * IB + t * P
                        jt = 2 * jp + 1 - s
                        pe.matmul(acc[:, t, 0:D + 1], ph[:, u, c:c + P], vtile(jt, 0, D + 1),
                                  start=(start and s == 0), stop=False)
                        pe.matmul(acc[:, t, 0:D], ph[:, u, c:c + P], vtile(jt, VLO, D),
                                  start=False, stop=False)
                        mm = pe.matmul(acc[:, t, 0:D + 1], pl[:, u, c:c + P], vtile(jt, 0, D + 1),
                                       start=False, stop=(stop and s == 1))
                mm.then_inc(pv_ok, 1)

            pe.wait_ge(xt_hi, KD * NB)
            pe.wait_ge(xt_lo, KD * NB)
            pe.wait_ge(ones_col, 1)
            pe.wait_ge(b1c_ok, 1)
            for u in range(2):
                scores(0, 0, u, first=True)

            def attention(b, first=False, last=False):
                for u in range(2):
                    scores(b, 1, u)
                    pv(b, u, u, start=(u == 0), fresh=first)
                with pe.Fori(1, NP // 2 - 1) as h:
                    for u in range(2):
                        scores(b, h + 1, u)
                        pv(b, 2 * h + u, u)
                for u in range(2):
                    if not last:
                        scores(b + 1, 0, u)
                    pv(b, NP - 2 + u, u, stop=(u == 1))

            attention(0, first=True)
            with pe.Fori(1, NB - 1) as b:
                attention(b)
            attention(NB - 1, last=True)

            def h_transposes(n):
                if n % 2 == 0:
                    pe.wait_ge(epi_ok, n // 2 + 1)
                if n >= 2:
                    pe.wait_ge(ht_hi, n - 1)
                    pe.wait_ge(ht_lo, n - 1)
                else:
                    pe.wait_ge(z_ok, NB * NP)
                for part, src in enumerate((xtTh, xtTl)):
                    for k in range(KD):
                        for s in range(2):
                            at = (part * KD + k) * 2 * P + s * P
                            mm = pe.transpose(sc16[:, n % 2, 0, at:at + P],
                                              src[:, (2 * n + s) * D + k * P:(2 * n + s) * D + k * P + P],
                                              ident[:, :])
                mm.then_inc(ht_ok, 1)
            for n in range(2 * NB - 2):
                h_transposes(n)

            pe.wait_ge(epi_ok, NB)
            pe.wait_ge(consts, 7)
            pe.wait_ge(hs_ok, NB)
            pe.wait_ge(acc_out, NT)
            for k in range(KD):
                mm = pe.matmul(acc[:, 0, k:k + 1], hsum[:, k * P:(k + 1) * P], tcol[:, :], start=True, stop=True)
            mm.then_inc(hmean_ok, 1)
            for n in range(2 * NB - 2, 2 * NB):
                h_transposes(n)
            pe.wait_ge(meanT_ok, KD)
            for k in range(KD):
                mm = pe.matmul(acc[:, 1, 0:E], meanB[:, k, :], gate[:, k, :], start=(k == 0), stop=(k == KD - 1))
            mm.then_inc(logit_ok, 1)

            def up(b, q, u, n, loaded=False, first=False):
                if not first:
                    pe.wait_ge(gelu_ok, 2 * n - 2)
                if not loaded:
                    pe.wait_ge(w1_hi, q + 1)
                    pe.wait_ge(w1_lo, q + 1)
                for s in range(2):
                    for i, (wm, hm) in enumerate(((w1h, xnTh), (w1l, xnTh), (w1h, xnTl))):
                        for k in range(KD):
                            mm = pe.matmul(sc[:, u, s, :], wm[:, q, k, s * P:(s + 1) * P], tr(hm, b, k, 0, IB),
                                           start=(i == 0 and k == 0), stop=(i == 2 and k == KD - 1))
                mm.then_inc(up_ok, 1)

            def down(b, q, u, n, loaded=False, fresh=False):
                pe.wait_ge(g_ok, n + 1)
                if not loaded:
                    pe.wait_ge(w2_hi, q + 1)
                    pe.wait_ge(w2_lo, q + 1)
                for t in range(TB):
                    if q == 0 and not fresh:
                        pe.wait_ge(y_out, TB * (b - 1) + t + 1)
                    for s in range(2):
                        c = s * IB + t * P
                        pe.matmul(acc[:, t, 0:D], ph[:, u, c:c + P], w2h[:, q, s, :],
                                  start=(q == 0 and s == 0), stop=False)
                        pe.matmul(acc[:, t, 0:D], ph[:, u, c:c + P], w2l[:, q, s, :], start=False, stop=False)
                        mm = pe.matmul(acc[:, t, 0:D], pl[:, u, c:c + P], w2h[:, q, s, :],
                                       start=False, stop=(q == NQ - 1 and s == 1))
                mm.then_inc(down_ok, 1)

            def ffn(b, first=False, last=False):
                for q in range(NQ):
                    n = b * NQ + q
                    if q + 2 < NQ:
                        up(b, q + 2, q % 2, n + 2, loaded=not first)
                    elif not last:
                        up(b + 1, q + 2 - NQ, q % 2, n + 2, loaded=True)
                    down(b, q, q % 2, n, loaded=not first, fresh=first)

            pe.wait_ge(ht_hi, 2 * NB)
            pe.wait_ge(ht_lo, 2 * NB)
            for q in range(2):
                up(0, q, q, q, first=True)
            ffn(0, first=True)
            with pe.Fori(1, NB - 1) as b:
                ffn(b)
            ffn(NB - 1, last=True)

        @block.scalar
        def _(act):
            act.wait_ge(w_in, 16)
            act.activation(Wh[:, :, :], Wf[:, :, :], ACT.Copy, scale=WSCALE).then_inc(w_hi, 1)
            for g in range(NB):
                act.wait_ge(xn_ok, g + 1)
                act.activation(vblock(g, 0, D), xn_f[:, g % 2], ACT.Copy).then_inc(vh_ok, 1)
                if g < 4:
                    act.wait_ge(iota_ok, g + 1)
                    act.activation(lw[:, g * LWC:(g + 1) * LWC], lw[:, g * LWC:(g + 1) * LWC], ACT.Abs).then_inc(labs_ok, 1)
                for n in range(2 * g, 2 * g + 2):
                    act.wait_ge(tp_ok, n + 1)
                    act.activation(bass.AP(xnTh, g * BLK + (n % 2) * 2 * P, [[NB * BLK, P], [IB, KD], [1, 2 * P]]),
                                   acc16[:, n % 2, 0:KD * 2 * P].rearrange("p (k c) -> p k c", k=KD),
                                   ACT.Copy).then_inc(tp_hi, 1)
                    act.activation(bass.AP(xnTl, g * BLK + (n % 2) * 2 * P, [[NB * BLK, P], [IB, KD], [1, 2 * P]]),
                                   acc16[:, n % 2, KD * 2 * P:2 * KD * 2 * P].rearrange("p (k c) -> p k c", k=KD),
                                   ACT.Copy).then_inc(tp_lo, 1)
                act.wait_ge(xt_ok, g + 1)
                if g == 0:
                    act.wait_ge(small_in, 48)
                for m in range(KD):
                    act.activation(tr(xtTh, g, m, 0, IB), sc[:, g % 2, m, :], ACT.Identity,
                                   bias=bcol[:, m:m + 1], scale=1.0 / WSCALE).then_inc(xt_hi, 1)
            act.wait_ge(b1t_ok, 1)
            act.activation(b1cols[:, :], acc[:, 2, 0:E * FT], ACT.Copy).then_inc(b1c_ok, 1)

            def softexp(n, u, fresh=False):
                act.wait_ge(z_ok, n + 1)
                act.activation(zbuf[:, u], zbuf[:, u], ACT.Tanh).then_inc(tanh_ok, 1)
                act.wait_ge(tanh_ok, n + 1)
                if not fresh:
                    act.wait_ge(p_ok, n - 1)
                act.activation(ebuf[:, u], zbuf[:, u], ACT.Exp).then_inc(exp_ok, 1)

            def drain(b):
                act.wait_ge(pv_ok, NP * (b + 1))
                if not isinstance(b, int) or b > 0:
                    act.wait_ge(epi_ok, b)
                for t in range(TB):
                    act.activation(accs[:, t, :], acc[:, t, 0:D + 1], ACT.Copy).then_inc(acc_out, 1)

            for u in range(2):
                softexp(u, u, fresh=True)

            def keep_x1(b):
                act.wait_ge(ec, EC * b + 8 + TB)
                act.activation(bass.AP(xres, b * TB * D, [[NT * D, P], [D, TB], [1, D]]), accs[:, :, 0:D],
                               ACT.Copy).then_inc(x1_kept, 1)

            def attention(b, first=False, last=False):
                with act.Fori(1, 4) as h:
                    for u in range(2):
                        softexp(b * NP + 2 * h + u, u)
                if not first:
                    keep_x1(b - 1)
                with act.Fori(4, NP // 2) as h:
                    for u in range(2):
                        softexp(b * NP + 2 * h + u, u)
                if not last:
                    for u in range(2):
                        softexp((b + 1) * NP + u, u)
                drain(b)

            attention(0, first=True)
            with act.Fori(1, NB - 1) as b:
                attention(b)
            attention(NB - 1, last=True)

            def copy_hT(n):
                act.wait_ge(ht_ok, n + 1)
                act.activation(bass.AP(xnTh, (n // 2) * BLK + (n % 2) * 2 * P, [[NB * BLK, P], [IB, KD], [1, 2 * P]]),
                               sc16[:, n % 2, 0, 0:KD * 2 * P].rearrange("p (k c) -> p k c", k=KD),
                               ACT.Copy).then_inc(ht_hi, 1)
                act.activation(bass.AP(xnTl, (n // 2) * BLK + (n % 2) * 2 * P, [[NB * BLK, P], [IB, KD], [1, 2 * P]]),
                               sc16[:, n % 2, 0, KD * 2 * P:2 * KD * 2 * P].rearrange("p (k c) -> p k c", k=KD),
                               ACT.Copy).then_inc(ht_lo, 1)
            for n in range(2 * NB):
                if n == 6:
                    keep_x1(NB - 1)
                copy_hT(n)
            act.wait_ge(lmax_ok, 1)
            act.activation(rt[:, 0, :], acc[:, 1, 0:E], ACT.Exp, bias=rc[:, 1:2]).then_inc(lexp_ok, 1)

            def weights_hi(q):
                act.wait_ge(w1_in[q], 16)
                act.activation(w1h[:, q], w1f[:, q], ACT.Copy, scale=WSCALE).then_inc(w1_hi, 1)
                act.wait_ge(w2_sc, q + 1)
                act.activation(w2h[:, q], w2f[:, q], ACT.Copy).then_inc(w2_hi, 1)

            def gelus(q, u, n, fresh=False):
                act.wait_ge(up_ok, n + 1)
                if not fresh:
                    act.wait_ge(g_ok, n - 1)
                for s in range(2):
                    act.activation(ebuf[:, u, s * IB:(s + 1) * IB], sc[:, u, s, :], ACT.Gelu,
                                   bias=b1sel[:, 2 * q + s:2 * q + s + 1], scale=1.0 / WSCALE).then_inc(gelu_ok, 1)

            def ffn(b, last=False):
                for q in range(2, NQ):
                    gelus(q, q % 2, b * NQ + q)
                if not last:
                    for q in range(2):
                        gelus(q, q, (b + 1) * NQ + q)
                act.wait_ge(down_ok, NQ * (b + 1))
                act.wait_ge(fin_ok, b)
                for t in range(TB):
                    act.activation(accs[:, t, 0:D], acc[:, t, 0:D], ACT.Copy, scale=1.0 / WSCALE).then_inc(y_out, 1)

            for q in range(2):
                weights_hi(q)
            act.wait_ge(b1sel_ok, TOP)
            for q in range(NQ):
                if q + 2 < NQ:
                    weights_hi(q + 2)
                gelus(q, q % 2, q, fresh=(q < 2))
            for q in range(2):
                gelus(q, q, NQ + q)
            act.wait_ge(down_ok, NQ)
            for t in range(TB):
                act.activation(accs[:, t, 0:D], acc[:, t, 0:D], ACT.Copy, scale=1.0 / WSCALE).then_inc(y_out, 1)
            with act.Fori(1, NB - 1) as b:
                ffn(b)
            ffn(NB - 1, last=True)

        @block.vector
        def _(ve):
            def norm_stats(src, n, u):
                if not isinstance(n, int) or n > 0:
                    ve.wait_ge(mv_ok, TB * n)
                ve.nop(nofuse=True)
                for t in range(TB):
                    ve.bn_stats(stats[:, u, t, :], src(t)).then_inc(st_ok, 1)
                ve.wait_ge(st_ok, TB * n + TB)
                ve.nop(nofuse=True)
                for t in range(TB):
                    ve.bn_aggr(mv[:, u, t, :], stats[:, u, t, :]).then_inc(mv_ok, 1)
                ve.wait_ge(mv_ok, TB * n + TB)

            def norm_var(n, u):
                ve.tensor_scalar(vtmp[:, u, :], mv[:, u, :, 1], EPS_LN, None, ALU.add).then_inc(var_ok, 1)

            def xtile(g):
                return lambda t: xres[:, TB * g + t, :]

            def xt_low(g):
                for m in range(KD):
                    ve.wait_ge(xt_hi, KD * g + m + 1)
                    if g >= 1:
                        ve.wait_ge(xt_lo, KD * (g - 1) + m + 1)
                    ve.tensor_scalar(xtf[:, m, :], sc[:, g % 2, m, :], 1.0 / WSCALE, bcol[:, m:m + 1],
                                     ALU.mult, ALU.add).then_inc(xtf_ok, 1)
                    ve.wait_ge(xtf_ok, KD * g + m + 1)
                    ve.tensor_tensor(tr(xtTl, g, m, 0, IB), xtf[:, m, :], tr(xtTh, g, m, 0, IB),
                                     ALU.subtract).then_inc(xt_lo, 1)

            ve.wait_ge(x_in[0], 16)
            norm_stats(xtile(0), 0, 0)
            norm_var(0, 0)
            ve.wait_ge(w_in, 16)
            ve.wait_ge(w_hi, 1)
            ve.scalar_tensor_tensor(out=Wl[:, :, :], in0=Wf[:, :, :], scalar=WSCALE, in1=Wh[:, :, :],
                                    op0=ALU.mult, op1=ALU.subtract).then_inc(w_lo, 1)
            for g in range(NB):
                u = g % 2
                if g + 1 < NB:
                    ve.wait_ge(x_in[g + 1], 16)
                    if g >= 1:
                        ve.wait_ge(xn_ok, g)
                    norm_stats(xtile(g + 1), g + 1, 1 - u)
                    norm_var(g + 1, 1 - u)
                ve.wait_ge(rstd_ok, g + 1)
                if g >= 2:
                    ve.wait_ge(vl_ok, g - 1)
                for t in range(TB):
                    ins = ve.tensor_scalar(xn_f[:, u, t, :], xres[:, TB * g + t, :], mv[:, u, t, 0:1],
                                           rstd[:, u, t:t + 1], ALU.subtract, ALU.mult)
                ins.then_inc(xn_ok, 1)
                if g >= 1:
                    xt_low(g - 1)
                if g >= 2 and g < 6:
                    ve.wait_ge(leps_ok, g - 1)
                    chunk = lw[:, (g - 2) * LWC:(g - 1) * LWC]
                    ve.reciprocal(chunk, chunk).then_inc(lrcp_ok, 1)
            xt_low(NB - 1)

            def weigh(b, jp, u):
                ve.wait_ge(scores_ok, b * NP + jp + 1)
                ve.tensor_tensor(zbuf[:, u].rearrange("p (s c) -> p s c", s=2), sc[:, u], lwpair(b, jp),
                                 ALU.mult).then_inc(z_ok, 1)

            def split(n, u, fresh=False):
                ve.wait_ge(exp_ok, n + 1)
                if not fresh:
                    ve.wait_ge(pv_ok, n - 1)
                ve.tensor_copy(ph[:, u], ebuf[:, u]).then_inc(phi_ok, 1)
                ve.wait_ge(phi_ok, n + 1)
                ve.tensor_tensor(pl[:, u], ebuf[:, u], ph[:, u], ALU.subtract).then_inc(p_ok, 1)

            accd = accs[:, :, 0:D]

            def epi_diag_hi(b):
                ve.wait_ge(acc_out, TB * (b + 1))
                ve.tensor_scalar(den[:, :], accs[:, :, D], -1.0, EPS_W, ALU.add, ALU.add).then_inc(ec, 1)
                ve.tensor_tensor(accd, accd, vblock(b, 0, D), ALU.subtract).then_inc(ec, 1)

            def epi_diag_lo(b):
                ve.wait_ge(ec, EC * b + 2)
                ve.reciprocal(rden[:, :], den[:, :]).then_inc(ec, 1)
                ve.tensor_tensor(accd, accd, vblock(b, VLO, D), ALU.subtract).then_inc(ec, 1)

            def epi_att_stats(b):
                ve.wait_ge(ec, EC * b + 4)
                norm_stats(lambda t: accs[:, t, 0:D], NB + 2 * b, 0)

            def epi_att_var(b):
                ve.tensor_tensor(vsc[:, 0, :], mv[:, 0, :, 1], rden[:, :], ALU.mult).then_inc(ec, 1)
                ve.wait_ge(ec, EC * b + 5)
                ve.tensor_tensor(vsc[:, 1, :], vsc[:, 0, :], rden[:, :], ALU.mult).then_inc(ec, 1)
                ve.wait_ge(ec, EC * b + 6)
                ve.tensor_scalar(vtmp[:, 0, :], vsc[:, 1, :], EPS_LN, None, ALU.add).then_inc(var_ok, 1)

            def epi_att_norm(b):
                ve.wait_ge(rstd_ok, NB + 2 * b + 1)
                ve.tensor_tensor(kfac[:, :], rstd[:, 0, :], rden[:, :], ALU.mult).then_inc(ec, 1)
                ve.wait_ge(ec, EC * b + 7)
                for t in range(TB):
                    ve.tensor_scalar(accs[:, t, 0:D], accs[:, t, 0:D], mv[:, 0, t, 0:1], kfac[:, t:t + 1],
                                     ALU.subtract, ALU.mult).then_inc(ec, 1)

            def epi_x1(b):
                ve.wait_ge(ec, EC * b + 7 + TB)
                x = bass.AP(xres, b * TB * D, [[NT * D, P], [D, TB], [1, D]])
                ve.tensor_tensor(accd, x, accd, ALU.add).then_inc(ec, 1)

            def epi_x1_stats(b):
                ve.wait_ge(ec, EC * b + 8 + TB)
                norm_stats(lambda t: accs[:, t, 0:D], NB + 2 * b + 1, 1)
                norm_var(NB + 2 * b + 1, 1)

            def epi_h(b):
                ve.wait_ge(rstd_ok, NB + 2 * b + 2)
                ve.wait_ge(x1_kept, b + 1)
                for t in range(TB):
                    ve.tensor_scalar(accs[:, t, 0:D], accs[:, t, 0:D],
                                     mv[:, 1, t, 0:1], rstd[:, 1, t:t + 1], ALU.subtract, ALU.mult).then_inc(ec, 1)

            def epi_h_sum(b):
                ve.wait_ge(ec, EC * b + 8 + 2 * TB)
                ve.tensor_reduce(htot[:, :], accs[:, :, 0:D].rearrange("p t d -> p d t"), AX_X, ALU.add).then_inc(ec, 1)
                hh = bass.AP(xtTh, b * BLK, [[NB * BLK, P], [D, TB], [1, D]])
                ve.tensor_copy(hh, accd).then_inc(ec, 1)
                ve.wait_ge(ec, EC * b + 10 + 2 * TB)

            def epi_h_lo(b):
                ve.wait_ge(ec, EC * (b + 1))
                hh = bass.AP(xtTh, b * BLK, [[NB * BLK, P], [D, TB], [1, D]])
                hl = bass.AP(xtTl, b * BLK, [[NB * BLK, P], [D, TB], [1, D]])
                ve.tensor_tensor(hsum[:, :], hsum[:, :], htot[:, :], ALU.add).then_inc(hs_ok, 1)
                ve.tensor_tensor(hl, accd, hh, ALU.subtract).then_inc(epi_ok, 1)

            def attention(b, first=False, last=False):
                for jp in range(2, 10):
                    weigh(b, jp, jp % 2)
                    split(b * NP + jp - 1, (jp - 1) % 2, fresh=(first and jp <= 2))
                    if first:
                        continue
                    if jp == 2:
                        epi_diag_hi(b - 1)
                    if jp == 3:
                        epi_diag_lo(b - 1)
                    if jp == 4:
                        epi_att_stats(b - 1)
                        epi_att_var(b - 1)
                    if jp == 5:
                        epi_att_norm(b - 1)
                    if jp == 6:
                        epi_x1(b - 1)
                    if jp == 7:
                        epi_x1_stats(b - 1)
                    if jp == 8:
                        epi_h(b - 1)
                    if jp == 9:
                        epi_h_sum(b - 1)
                        epi_h_lo(b - 1)
                with ve.Fori(5, NP // 2) as h:
                    for u in range(2):
                        weigh(b, 2 * h + u, u)
                        split(b * NP + 2 * h + u - 1, 1 - u)
                for jp in range(2):
                    if not last:
                        weigh(b + 1, jp, jp)
                    if jp == 0 or not last:
                        split(b * NP + NP + jp - 1, 1 - jp)

            ve.wait_ge(consts, 7)
            ve.wait_ge(lw_ok, 1)
            weigh(0, 0, 0)
            weigh(0, 1, 1)
            split(0, 0, fresh=True)
            attention(0, first=True)
            with ve.Fori(1, NB - 1) as b:
                attention(b)
            attention(NB - 1, last=True)
            epi_diag_hi(NB - 1)
            epi_diag_lo(NB - 1)
            epi_att_stats(NB - 1)
            epi_att_var(NB - 1)
            epi_att_norm(NB - 1)
            epi_x1(NB - 1)
            epi_x1_stats(NB - 1)
            epi_h(NB - 1)
            epi_h_sum(NB - 1)
            epi_h_lo(NB - 1)

            links = [0]

            def link(ins):
                links[0] += 1
                ins.then_inc(rchain, 1)
                ve.wait_ge(rchain, links[0])
            LMAX, NLMAX, ESUM, ERCP, P1, R1, P2, R2, PS, PR, C1, C2 = (rc[:, i:i + 1] for i in range(12))
            EXPS, PROBS, CAND1, ONE1, REST, CAND2, ONE2, COMB1 = (rt[:, i, :] for i in range(8))
            ve.wait_ge(hmean_ok, 1)
            link(ve.tensor_copy(meanT[:, :], acc[:, 0, 0:KD]))
            for k in range(KD):
                ve.tensor_scalar(meanB[:, k, :], ones[:, :], meanT[:, k:k + 1], None, ALU.mult).then_inc(meanT_ok, 1)
            ve.wait_ge(logit_ok, 1)
            link(ve.tensor_reduce(LMAX, acc[:, 1, 0:E], AX_X, ALU.max))
            ve.tensor_scalar(NLMAX, LMAX, -1.0, None, ALU.mult).then_inc(lmax_ok, 1)
            ve.wait_ge(lexp_ok, 1)
            link(ve.tensor_reduce(ESUM, EXPS, AX_X, ALU.add))
            link(ve.reciprocal(ERCP, ESUM))
            link(ve.tensor_scalar(PROBS, EXPS, ERCP, None, ALU.mult))
            link(ve.tensor_reduce(P1, PROBS, AX_X, ALU.max))
            link(ve.scalar_tensor_tensor(out=CAND1, in0=PROBS, scalar=P1, in1=rev[:, :],
                                         op0=ALU.is_equal, op1=ALU.mult))
            link(ve.tensor_reduce(R1, CAND1, AX_X, ALU.max))
            link(ve.tensor_scalar(ONE1, rev[:, :], R1, None, ALU.is_equal))
            link(ve.scalar_tensor_tensor(out=REST, in0=ONE1, scalar=-2.0, in1=PROBS, op0=ALU.mult, op1=ALU.add))
            link(ve.tensor_reduce(P2, REST, AX_X, ALU.max))
            link(ve.scalar_tensor_tensor(out=CAND2, in0=REST, scalar=P2, in1=rev[:, :],
                                         op0=ALU.is_equal, op1=ALU.mult))
            link(ve.tensor_reduce(R2, CAND2, AX_X, ALU.max))
            ve.tensor_scalar(eidx[:, 0:1], R1, -1.0, float(E), ALU.mult, ALU.add).then_inc(route_ok, 1)
            ve.tensor_scalar(eidx[:, 1:2], R2, -1.0, float(E), ALU.mult, ALU.add).then_inc(route_ok, 1)
            link(ve.tensor_scalar(ONE2, rev[:, :], R2, None, ALU.is_equal))
            link(ve.tensor_tensor(PS, P1, P2, ALU.add))
            link(ve.reciprocal(PR, PS))
            link(ve.tensor_tensor(C1, P1, PR, ALU.mult))
            link(ve.tensor_tensor(C2, P2, PR, ALU.mult))
            link(ve.tensor_scalar(COMB1, ONE1, C1, None, ALU.mult))
            link(ve.scalar_tensor_tensor(out=comb[:, :], in0=ONE2, scalar=C2, in1=COMB1, op0=ALU.mult, op1=ALU.add))
            for i, one in enumerate((ONE1, ONE2)):
                link(ve.tensor_tensor(bprod[:, i], b1cols[:, :].rearrange("p (e t) -> p t e", e=E),
                                      one.unsqueeze(1).broadcast_to([P, FT, E]), ALU.mult))
                ve.tensor_reduce(b1sel[:, i * FT:(i + 1) * FT], bprod[:, i], AX_X, ALU.add).then_inc(b1sel_ok, 1)

            def w2_scale(q):
                ve.wait_ge(w2_in[q], 16)
                ve.tensor_scalar(w2f[:, q], w2f[:, q], (C1, C2)[q // FP], WSCALE, ALU.mult, ALU.mult).then_inc(w2_sc, 1)

            def weights_lo(q):
                ve.wait_ge(w1_hi, q + 1)
                ve.scalar_tensor_tensor(out=w1l[:, q], in0=w1f[:, q], scalar=WSCALE, in1=w1h[:, q],
                                        op0=ALU.mult, op1=ALU.subtract).then_inc(w1_lo, 1)
                ve.wait_ge(w2_hi, q + 1)
                ve.tensor_tensor(w2l[:, q], w2f[:, q], w2h[:, q], ALU.subtract).then_inc(w2_lo, 1)

            def gsplit(n, u, fresh=False):
                ve.wait_ge(gelu_ok, 2 * n + 2)
                if not fresh:
                    ve.wait_ge(down_ok, n - 1)
                ve.tensor_copy(ph[:, u], ebuf[:, u]).then_inc(ghi_ok, 1)
                ve.wait_ge(ghi_ok, n + 1)
                ve.tensor_tensor(pl[:, u], ebuf[:, u], ph[:, u], ALU.subtract).then_inc(g_ok, 1)

            def fin_bias(b):
                ve.wait_ge(y_out, TB * (b + 1))
                ve.tensor_tensor(accd, accd, b2c[:, :].unsqueeze(1).broadcast_to([P, TB, D]), ALU.add).then_inc(fc, 1)

            def fin_stats(b):
                ve.wait_ge(fc, (TB + 1) * b + 1)
                norm_stats(lambda t: accs[:, t, 0:D], 3 * NB + b, 0)
                norm_var(3 * NB + b, 0)

            def fin_norm(b):
                ve.wait_ge(rstd_ok, 3 * NB + b + 1)
                for t in range(TB):
                    ve.tensor_scalar(accs[:, t, 0:D], accs[:, t, 0:D], mv[:, 0, t, 0:1], rstd[:, 0, t:t + 1],
                                     ALU.subtract, ALU.mult).then_inc(fc, 1)

            def fin_add(b):
                ve.wait_ge(fc, (TB + 1) * (b + 1))
                x2 = bass.AP(xres, b * TB * D, [[NT * D, P], [D, TB], [1, D]])
                ve.tensor_tensor(x2, x2, accd, ALU.add).then_inc(fin_ok, 1)

            for q in range(2):
                w2_scale(q)
            for q in range(2):
                weights_lo(q)
            for q in range(NQ):
                if q + 2 < NQ:
                    w2_scale(q + 2)
                    weights_lo(q + 2)
                gsplit(q, q % 2, fresh=(q < 2))
                if q == 3:
                    ve.wait_ge(b2_in, 16)
                    link(ve.tensor_scalar(b2c[:, :], b2all[:, 0, :], comb[:, 0:1], None, ALU.mult))
                if q >= 4 and q < 4 + (E - 1 + 1) // 2:
                    for e in range(1 + 2 * (q - 4), min(3 + 2 * (q - 4), E)):
                        link(ve.scalar_tensor_tensor(out=b2c[:, :], in0=b2all[:, e, :], scalar=comb[:, e:e + 1],
                                                     in1=b2c[:, :], op0=ALU.mult, op1=ALU.add))

            def ffn(b):
                for q in range(NQ):
                    gsplit(b * NQ + q, q % 2)
                    if q == 2:
                        fin_bias(b - 1)
                    if q == 3:
                        fin_stats(b - 1)
                    if q == 4:
                        fin_norm(b - 1)
                    if q == 5:
                        fin_add(b - 1)
            with ve.Fori(1, NB) as b:
                ffn(b)
            fin_bias(NB - 1)
            fin_stats(NB - 1)
            fin_norm(NB - 1)
            fin_add(NB - 1)


_INS = ['L0_attn_x', 'L0_attn_W', 'L0_attn_b', 'L0_ffn_gate_w', 'L0_ffn_w1', 'L0_ffn_b1', 'L0_ffn_w2', 'L0_ffn_b2']
_OUTS = [((1, 4096, 256), 'float32')]


def kernel(**inputs):
    import numpy as _np
    import concourse.bacc as _bacc
    from concourse import mybir as _mybir
    from concourse.bass_utils import run_bass_kernel_spmd as _run

    nc = _bacc.Bacc("TRN2", target_bir_lowering=False, num_devices=1)
    arrays, args = {}, []
    for name in _INS:
        a = _np.ascontiguousarray(inputs[name])
        arrays[f"in_{name}_dram"] = a
        args.append(nc.dram_tensor(f"in_{name}_dram", a.shape, _mybir.dt.from_np(a.dtype), kind="ExternalInput").ap())
    for i, (shape, dtype) in enumerate(_OUTS):
        dt = _mybir.dt.from_np(_np.dtype(dtype))
        args.append(nc.dram_tensor(f"out_{i}_dram", shape, dt, kind="ExternalOutput").ap())
    program(nc, *args)
    r = _run(nc, [arrays], core_ids=[0])
    return r.results[0]["out_0_dram"]
```

```python
from contextlib import ExitStack

import concourse.bass as bass
from concourse import mybir

ALU = mybir.AluOpType
ACT = mybir.ActivationFunctionType
AX_X = mybir.AxisListType.X
F32 = mybir.dt.float32
F16 = mybir.dt.float16
I32 = mybir.dt.int32

P = 128
EPS_LN = 1e-5
EPS_W = 1e-7
WSCALE = 16.0
TOP = 2


def program(nc, x_d, W_d, b_d, gate_d, w1_d, b1_d, w2_d, b2_d, out_d):
    _, S, D = x_d.shape
    E, _, F = w1_d.shape
    KD = D // P
    NT = S // P
    IB = 512
    TB = IB // P
    NB = S // IB
    NP = NT // 2
    BLK = KD * IB
    VW = 2 * D + 2
    VLO = D + 2
    LWOFF = S - 1
    LWW = 2 * S - P
    LW0 = LWOFF - (IB - 1)
    LWCUT = (LW0, LW0 + LWW // 4, LWW)
    LC = 2 * S // P
    FT = F // P
    FP = FT // 2
    NQ = TOP * FP
    FC = 2 * P
    LWA = max(LWW, NQ * (KD * FC + 2 * D))
    EC = 10 + 2 * TB

    with ExitStack() as ctx:
        def sb(name, shape, dt=F32):
            return ctx.enter_context(nc.sbuf_tensor(name, shape, dt))

        def sem(name):
            return ctx.enter_context(nc.semaphore(name))

        xres = sb("xres", [P, NT, D])
        lw = sb("lw", [P, LWA])
        vmat = sb("vmat", [P, NT * VW], F16)
        xnTh = sb("xnTh", [P, NB * BLK], F16)
        xnTl = sb("xnTl", [P, NB * BLK], F16)
        xtTh = sb("xtTh", [P, NB * BLK], F16)
        xtTl = sb("xtTl", [P, NB * BLK], F16)
        zbuf = sb("zbuf", [P, 2, 2 * IB])
        ebuf = sb("ebuf", [P, 2, 2 * IB])
        ph = sb("ph", [P, 2, 2 * IB], F16)
        pl = sb("pl", [P, 2, 2 * IB], F16)
        accs = sb("accs", [P, TB, D + 1])
        hsum = sb("hsum", [P, D])
        bprod = sb("bprod", [P, TOP, FT, E])
        ltoe = sb("ltoe", [P, 4, LC])
        xn_f = sb("xn_f", [P, 2, TB, D])
        Wh = sb("Wh", [P, KD, D], F16)
        Wl = sb("Wl", [P, KD, D], F16)
        bcol = sb("bcol", [P, KD])
        gate = sb("gate", [P, KD, E])
        b1rows = sb("b1rows", [E * FT, P])
        b1cols = sb("b1cols", [P, E * FT])
        b1sel = sb("b1sel", [P, TOP * FT])
        ident = sb("ident", [P, P], F16)
        identf = sb("identf", [P, P])
        ones = sb("ones", [P, P])
        tcol = sb("tcol", [P, 1])
        half = sb("half", [P, 2 * TB])
        stats = sb("stats", [P, 2, TB, 6])
        mv = sb("mv", [P, 2, TB, 2])
        rstd = sb("rstd", [P, 2, TB])
        rden = sb("rden", [P, TB])
        den = sb("den", [P, TB])
        kfac = sb("kfac", [P, TB])
        vsc = sb("vsc", [P, 2, TB])
        htot = sb("htot", [P, D])
        vtmp = sb("vtmp", [P, 2, TB])
        meanT = sb("meanT", [P, KD])
        meanB = sb("meanB", [P, KD, P])
        rt = sb("rt", [P, 12, E])
        rc = sb("rc", [P, 16])
        rev = sb("rev", [P, E])
        eidx = sb("eidx", [P, TOP], I32)
        comb = sb("comb", [P, E])
        b2c = sb("b2c", [P, D])

        Wf = zbuf[:, 0, 0:KD * D].rearrange("p (k n) -> p k n", k=KD)
        xtf = accs[:, :, :].rearrange("p t w -> p (t w)")[:, 0:BLK]
        b2all = xn_f[:, :, :, :].rearrange("p u t d -> p (u t) d")
        w1f = lw[:, 0:NQ * KD * FC].rearrange("p (q k f) -> p q k f", q=NQ, k=KD)
        w2f = lw[:, NQ * KD * FC:NQ * KD * FC + NQ * 2 * D].rearrange("p (q s d) -> p q s d", q=NQ, s=2)
        n_w = NQ * KD * FC

        def wview(n):
            return vmat[:, n * n_w:(n + 1) * n_w].rearrange("p (q k f) -> p q k f", q=NQ, k=2)
        w1h, w1l, w2h, w2l = (wview(n) for n in range(4))

        sc = ctx.enter_context(nc.psum_tensor("sc", [P, 2, 2, IB], F32))
        acc = ctx.enter_context(nc.psum_tensor("acc", [P, TB, 512], F32))

        x_in = [sem(f"x_in{g}") for g in range(3)]
        xrest_in = sem("xrest_in")
        w_in = sem("w_in")
        small_in = sem("small_in")
        b2_in = sem("b2_in")
        lchain = sem("lchain")
        ltoe_ok = sem("ltoe_ok")
        lflat_out = sem("lflat_out")
        lw_in = [sem(f"lw_in{c}") for c in range(3)]
        consts = sem("consts")
        ident_ok = sem("ident_ok")
        iota_ok = sem("iota_ok")
        ones_col = sem("ones_col")
        st_ok = sem("st_ok")
        mv_ok = sem("mv_ok")
        xtf_ok = sem("xtf_ok")
        ec = sem("ec")
        x1_kept = sem("x1_kept")
        hs_ok = sem("hs_ok")
        rchain = sem("rchain")
        fc = sem("fc")
        var_ok = sem("var_ok")
        rstd_ok = sem("rstd_ok")
        xn_ok = sem("xn_ok")
        vh_ok = sem("vh_ok")
        vl_ok = sem("vl_ok")
        w_hi = sem("w_hi")
        w_lo = sem("w_lo")
        tp_ok = sem("tp_ok")
        tp_hi = sem("tp_hi")
        tp_lo = sem("tp_lo")
        xt_ok = sem("xt_ok")
        xt_hi = sem("xt_hi")
        xt_lo = sem("xt_lo")
        scores_ok = sem("scores_ok")
        z_ok = sem("z_ok")
        tanh_ok = sem("tanh_ok")
        exp_ok = sem("exp_ok")
        phi_ok = sem("phi_ok")
        p_ok = sem("p_ok")
        pv_ok = sem("pv_ok")
        acc_out = sem("acc_out")
        epi_ok = sem("epi_ok")
        b1t_ok = sem("b1t_ok")
        b1c_ok = sem("b1c_ok")
        hmean_ok = sem("hmean_ok")
        meanT_ok = sem("meanT_ok")
        logit_ok = sem("logit_ok")
        lmax_ok = sem("lmax_ok")
        lexp_ok = sem("lexp_ok")
        route_ok = sem("route_ok")
        w1_in = [sem(f"w1_in{q}") for q in range(NQ)]
        w2_in = [sem(f"w2_in{q}") for q in range(NQ)]
        b1sel_ok = sem("b1sel_ok")
        w1_hi = sem("w1_hi")
        w1_lo = sem("w1_lo")
        w2_sc = sem("w2_sc")
        w2_hi = sem("w2_hi")
        w2_lo = sem("w2_lo")
        ht_ok = sem("ht_ok")
        ht_hi = sem("ht_hi")
        ht_lo = sem("ht_lo")
        up_ok = sem("up_ok")
        gelu_ok = sem("gelu_ok")
        ghi_ok = sem("ghi_ok")
        g_ok = sem("g_ok")
        down_ok = sem("down_ok")
        y_out = sem("y_out")
        fin_ok = sem("fin_ok")
        store_ok = sem("store_ok")

        def vtile(t, lo, n):
            base = t * VW + lo
            return vmat[:, base:base + n] if isinstance(t, int) else vmat[:, bass.ds(base, n)]

        def vblock(g, lo, n):
            return bass.AP(vmat, g * TB * VW + lo, [[NT * VW, P], [VW, TB], [1, n]])

        def tr(buf, g, k, c, n):
            return buf[:, bass.ds(g * BLK + k * IB + c, n)]

        def lwpair(b, jp):
            return bass.AP(lw, b * -IB + jp * (2 * P) + LW0, [[LWA, P], [P, 2], [1, IB]])

        sc16 = sc[:, :, :, :].bitcast(F16)

        lflat = nc.dram_tensor("lflat", [1, 2 * S], F32, kind="Internal").ap()

        block = ctx.enter_context(nc.Block())

        @block.sync
        def _(sp):
            xv = x_d[0].rearrange("(g t p) d -> g p t d", t=TB, p=P)
            def load_x(g, landed):
                sp.dma_start(xres[:, TB * g:TB * g + TB, :], xv[g]).then_inc(landed, 16)

            def load_lw(part, c0, c1):
                sp.dma_start(lw[:, c0:c1], bass.AP(lflat.tensor, c0, [[1, P], [1, c1 - c0]])).then_inc(lw_in[part], 16)

            load_x(0, x_in[0])
            sp.dma_start(Wf[:, :, :], W_d.rearrange("(k p) n -> p k n", p=P)).then_inc(w_in, 16)
            load_x(1, x_in[1])
            sp.wait_ge(ltoe_ok, 1)
            sp.dma_start(lflat.rearrange("a (p c) -> (a p) c", p=P), ltoe[:, 3, :]).then_inc(lflat_out, 16)
            load_x(2, x_in[2])
            sp.wait_ge(lflat_out, 16)
            load_lw(0, LWCUT[0], LWCUT[1])
            for g in range(3, NB):
                load_x(g, xrest_in)
            load_lw(1, LWCUT[1], LWCUT[2])
            load_lw(2, 0, LWCUT[0])

            sp.wait_ge(route_ok, TOP)
            for e in range(TOP):
                ex = sp.value_load(eidx[0:1, e:e + 1], min_val=0, max_val=E - 1)
                for f in range(FP):
                    q = e * FP + f
                    sp.dma_start(w1f[:, q], w1_d[bass.ds(ex, 1), :, f * FC:(f + 1) * FC]
                                 .rearrange("a (k p) f -> p (a k) f", p=P)).then_inc(w1_in[q], 16)
                    sp.dma_start(w2f[:, q], w2_d[bass.ds(ex, 1), f * FC:(f + 1) * FC, :]
                                 .rearrange("a (s p) d -> p (a s) d", p=P)).then_inc(w2_in[q], 16)
            ov = out_d[0].rearrange("(g t p) d -> g p t d", t=TB, p=P)
            for g in range(NB):
                sp.wait_ge(fin_ok, g + 1)
                sp.dma_start(ov[g], xres[:, TB * g:TB * g + TB, :]).then_inc(store_ok, 16)
            sp.wait_ge(store_ok, 16 * NB)

        @block.gpsimd
        def _(pool):
            pool.iota(ltoe[:, 0, :], [[1, LC]], base=-LWOFF, channel_multiplier=LC,
                      allow_small_or_imprecise_dtypes=True).then_inc(iota_ok, 1)
            pool.memset(half[:, :], -0.5).then_inc(consts, 1)
            pool.memset(ident[:, :], 0.0).then_inc(consts, 1)
            pool.memset(identf[:, :], 0.0).then_inc(consts, 1)
            pool.wait_ge(consts, 3)
            for m in (ident, identf):
                pool.affine_select(out=m[:, :], in_=m[:, :], compare_op=ALU.not_equal, fill=1.0, base=0,
                                   pattern=[[-1, P]], channel_multiplier=1).then_inc(ident_ok, 1)
            pool.memset(vmat[:, :].rearrange("p (t w) -> p t w", w=VW)[:, :, D:D + 2], 1.0).then_inc(ones_col, 1)
            pool.memset(ones[:, :], 1.0).then_inc(consts, 1)
            pool.memset(tcol[:, :], 1.0 / S).then_inc(consts, 1)
            pool.memset(hsum[:, :], 0.0).then_inc(consts, 1)
            pool.iota(rev[:, :], [[-1, E]], base=E, channel_multiplier=0,
                      allow_small_or_imprecise_dtypes=True).then_inc(consts, 1)
            pool.dma_start(gate[:, :, :], gate_d.rearrange("(k p) e -> p k e", p=P)).then_inc(small_in, 16)
            pool.dma_start(bcol[:, :], b_d.rearrange("(k p) -> p k", p=P), allow_slow_non_contiguous=True).then_inc(small_in, 16)
            pool.dma_start(b1rows[:, :], b1_d.rearrange("e (t p) -> (e t) p", p=P)).then_inc(small_in, 16)

            def power(n, u):
                pool.wait_ge(var_ok, n + 1)
                pool.tensor_tensor(rstd[:, u, :], vtmp[:, u, :], half[:, 0:TB], ALU.pow).then_inc(rstd_ok, 1)

            def ln_x(g, u):
                power(g, u)
                pool.wait_ge(vh_ok, g + 1)
                pool.tensor_tensor(vblock(g, VLO, D), xn_f[:, u], vblock(g, 0, D),
                                   ALU.subtract).then_inc(vl_ok, 1)
            with pool.Fori(0, NB // 2) as m:
                for u in range(2):
                    ln_x(2 * m + u, u)
            pool.wait_ge(vh_ok, NB)
            pool.wait_ge(vl_ok, NB)
            pool.dma_start(b2all, bass.AP(b2_d.tensor, 0, [[0, P], [D, E], [1, D]])).then_inc(b2_in, 16)
            with pool.Fori(0, NB) as b:
                for u in range(2):
                    power(NB + 2 * b + u, u)
            with pool.Fori(0, NB) as b:
                power(3 * NB + b, 0)

        @block.tensor
        def _(pe):
            def transposes(g):
                pe.wait_ge(vh_ok, g + 1)
                pe.wait_ge(vl_ok, g + 1)
                if not isinstance(g, int) or g > 0:
                    pe.wait_ge(z_ok, 2 * g - 1)
                for part, lo in enumerate((0, VLO)):
                    for k in range(KD):
                        for t in range(TB):
                            mm = pe.transpose(sc16[:, 0, part, k * IB + t * P:k * IB + t * P + P],
                                              vtile(TB * g + t, lo + k * P, P), ident[:, :])
                mm.then_inc(tp_ok, 1)

            def xt_product(g):
                pe.wait_ge(tp_hi, g + 1)
                pe.wait_ge(tp_lo, g + 1)
                if not isinstance(g, int) or g > 0:
                    pe.wait_ge(z_ok, 2 * g)
                for m in range(KD):
                    for i, (wp, xp) in enumerate(((Wh, xnTh), (Wl, xnTh), (Wh, xnTl))):
                        for k in range(KD):
                            mm = pe.matmul(sc[:, 1, m, :], wp[:, k, m * P:(m + 1) * P], tr(xp, g, k, 0, IB),
                                           start=(i == 0 and k == 0), stop=(i == 2 and k == KD - 1))
                mm.then_inc(xt_ok, 1)

            def scores(b, h, u, wait_z=True):
                if wait_z:
                    pe.wait_ge(z_ok, b * NP + 2 * h + u - 1)
                for s in range(2):
                    for i, (jm, im) in enumerate(((xnTh, xtTh), (xnTl, xtTh), (xnTh, xtTl))):
                        for k in range(KD):
                            mm = pe.matmul(sc[:, u, s, :], tr(jm, h, k, (2 * u + s) * P, P), tr(im, b, k, 0, IB),
                                           start=(i == 0 and k == 0), stop=(i == 2 and k == KD - 1))
                mm.then_inc(scores_ok, 1)

            def pv(b, jp, u, start=False, stop=False, fresh=False):
                pe.wait_ge(p_ok, b * NP + jp + 1)
                for t in range(TB):
                    if start and not fresh:
                        pe.wait_ge(acc_out, TB * (b - 1) + t + 1)
                    for s in range(2):
                        jt = 2 * jp + s
                        pe.matmul(acc[:, t, 0:D + 1], ph[:, u, s * IB + t * P:s * IB + (t + 1) * P], vtile(jt, 0, D + 1),
                                  start=(start and s == 0), stop=False)
                        pe.matmul(acc[:, t, 0:D], ph[:, u, s * IB + t * P:s * IB + (t + 1) * P], vtile(jt, VLO, D),
                                  start=False, stop=False)
                        mm = pe.matmul(acc[:, t, 0:D + 1], pl[:, u, s * IB + t * P:s * IB + (t + 1) * P], vtile(jt, 0, D + 1),
                                       start=False, stop=(stop and s == 1))
                mm.then_inc(pv_ok, 1)

            def block0_step(g, u_last=None, first=False):
                transposes(g)
                if not first:
                    pv(0, 2 * g - 3, 1)
                pe.wait_ge(tp_hi, g + 1)
                pe.wait_ge(tp_lo, g + 1)
                scores(0, g, 0, wait_z=False)
                xt_product(g)
                pv(0, 2 * g - 2, 0, start=first, fresh=first)
                pe.wait_ge(xtf_ok, KD * (g + 1))
                scores(0, g, 1, wait_z=False)

            pe.wait_ge(ident_ok, 2)
            pe.wait_ge(ones_col, 1)
            transposes(0)
            pe.wait_ge(w_hi, 1)
            pe.wait_ge(w_lo, 1)
            xt_product(0)
            pe.wait_ge(xt_hi, 1)
            pe.wait_ge(xt_lo, 1)
            scores(0, 0, 0, wait_z=False)
            scores(0, 0, 1, wait_z=False)
            block0_step(1, first=True)
            with pe.Fori(2, NB) as g:
                block0_step(g)
            pv(0, NP - 3, 1)
            pe.wait_ge(xt_hi, NB)
            pe.wait_ge(xt_lo, NB)
            for u in range(2):
                scores(1, 0, u)
                pv(0, NP - 2 + u, u, stop=(u == 1))

            def attention(b, last=False):
                for u in range(2):
                    scores(b, 1, u)
                    pv(b, u, u, start=(u == 0))
                with pe.Fori(1, NP // 2 - 1) as h:
                    for u in range(2):
                        scores(b, h + 1, u)
                        pv(b, 2 * h + u, u)
                for u in range(2):
                    if not last:
                        scores(b + 1, 0, u)
                    pv(b, NP - 2 + u, u, stop=(u == 1))

            with pe.Fori(1, NB - 1) as b:
                attention(b)
            attention(NB - 1, last=True)

            def h_transposes(b):
                pe.wait_ge(epi_ok, b + 1)
                if b >= 2:
                    pe.wait_ge(ht_hi, b - 1)
                    pe.wait_ge(ht_lo, b - 1)
                for part, src in enumerate((xtTh, xtTl)):
                    for k in range(KD):
                        for t in range(TB):
                            at = b * BLK + t * D + k * P
                            mm = pe.transpose(sc16[:, b % 2, part, k * IB + t * P:k * IB + t * P + P],
                                              src[:, at:at + P], ident[:, :])
                mm.then_inc(ht_ok, 1)
            pe.wait_ge(z_ok, NB * NP)
            for b in range(NB - 3):
                h_transposes(b)

            pe.wait_ge(epi_ok, NB)
            pe.wait_ge(consts, 7)
            pe.wait_ge(small_in, 48)
            pe.wait_ge(hs_ok, NB)
            pe.wait_ge(acc_out, NT)
            for k in range(KD):
                mm = pe.matmul(acc[:, 0, k:k + 1], hsum[:, k * P:(k + 1) * P], tcol[:, :], start=True, stop=True)
            mm.then_inc(hmean_ok, 1)
            pe.wait_ge(meanT_ok, KD)
            for k in range(KD):
                mm = pe.matmul(acc[:, 1, 0:E], meanB[:, k, :], gate[:, k, :], start=(k == 0), stop=(k == KD - 1))
            mm.then_inc(logit_ok, 1)
            pe.transpose(acc[:, 2, 0:E * FT], b1rows[:, :], identf[0:E * FT, 0:E * FT]).then_inc(b1t_ok, 1)
            for b in range(NB - 3, NB):
                h_transposes(b)

            def up(b, q, u, n, loaded=False, first=False):
                if not first:
                    pe.wait_ge(gelu_ok, 2 * n - 2)
                if not loaded:
                    pe.wait_ge(w1_hi, q + 1)
                    pe.wait_ge(w1_lo, q + 1)
                for s in range(2):
                    for i, (wm, hm) in enumerate(((w1h, xnTh), (w1l, xnTh), (w1h, xnTl))):
                        for k in range(KD):
                            mm = pe.matmul(sc[:, u, s, :], wm[:, q, k, s * P:(s + 1) * P], tr(hm, b, k, 0, IB),
                                           start=(i == 0 and k == 0), stop=(i == 2 and k == KD - 1))
                mm.then_inc(up_ok, 1)

            def down(b, q, u, n, loaded=False, fresh=False):
                pe.wait_ge(g_ok, n + 1)
                if not loaded:
                    pe.wait_ge(w2_hi, q + 1)
                    pe.wait_ge(w2_lo, q + 1)
                for t in range(TB):
                    if q == 0 and not fresh:
                        pe.wait_ge(y_out, TB * (b - 1) + t + 1)
                    for s in range(2):
                        c = s * IB + t * P
                        pe.matmul(acc[:, t, 0:D], ph[:, u, c:c + P], w2h[:, q, s, :],
                                  start=(q == 0 and s == 0), stop=False)
                        pe.matmul(acc[:, t, 0:D], ph[:, u, c:c + P], w2l[:, q, s, :], start=False, stop=False)
                        mm = pe.matmul(acc[:, t, 0:D], pl[:, u, c:c + P], w2h[:, q, s, :],
                                       start=False, stop=(q == NQ - 1 and s == 1))
                mm.then_inc(down_ok, 1)

            def ffn(b, first=False, last=False):
                for q in range(NQ):
                    n = b * NQ + q
                    if q + 2 < NQ:
                        up(b, q + 2, q % 2, n + 2, loaded=not first)
                    elif not last:
                        up(b + 1, q + 2 - NQ, q % 2, n + 2, loaded=True)
                    down(b, q, q % 2, n, loaded=not first, fresh=first)

            pe.wait_ge(ht_hi, NB)
            pe.wait_ge(ht_lo, NB)
            for q in range(2):
                up(0, q, q, q, first=True)
            ffn(0, first=True)
            with pe.Fori(1, NB - 1) as b:
                ffn(b)
            ffn(NB - 1, last=True)

        @block.scalar
        def _(act):
            act.wait_ge(w_in, 16)
            act.activation(Wh[:, :, :], Wf[:, :, :], ACT.Copy, scale=WSCALE).then_inc(w_hi, 1)

            def v_hi(g, u):
                act.wait_ge(xn_ok, g + 1)
                act.activation(vblock(g, 0, D), xn_f[:, u], ACT.Copy).then_inc(vh_ok, 1)

            def copy_xnT(g):
                act.wait_ge(tp_ok, g + 1)
                act.activation(xnTh[:, bass.ds(g * BLK, BLK)], sc16[:, 0, 0, :], ACT.Copy).then_inc(tp_hi, 1)
                act.activation(xnTl[:, bass.ds(g * BLK, BLK)], sc16[:, 0, 1, :], ACT.Copy).then_inc(tp_lo, 1)

            def xt_bias(g):
                act.wait_ge(xt_ok, g + 1)
                if not isinstance(g, int) or g > 0:
                    act.wait_ge(xt_lo, g)
                for m in range(KD):
                    act.activation(bass.AP(accs, m * IB + IB - 1, [[TB * (D + 1), P], [-1, IB]]), sc[:, 1, m, :], ACT.Identity,
                                   bias=bcol[:, m:m + 1], scale=1.0 / WSCALE).then_inc(xtf_ok, 1)

            def softexp(n, u, fresh=False):
                act.wait_ge(z_ok, n + 1)
                act.activation(zbuf[:, u], zbuf[:, u], ACT.Tanh).then_inc(tanh_ok, 1)
                act.wait_ge(tanh_ok, n + 1)
                if not fresh:
                    act.wait_ge(p_ok, n - 1)
                act.activation(bass.AP(ebuf, u * 2 * IB + IB - 1, [[4 * IB, P], [IB, 2], [-1, IB]]),
                               zbuf[:, u].rearrange("p (s c) -> p s c", s=2), ACT.Exp).then_inc(exp_ok, 1)

            def drain(b):
                act.wait_ge(pv_ok, NP * (b + 1))
                if not isinstance(b, int) or b > 0:
                    act.wait_ge(epi_ok, b)
                for t in range(TB):
                    act.activation(accs[:, t, :], acc[:, t, 0:D + 1], ACT.Copy).then_inc(acc_out, 1)

            v_hi(0, 0)
            copy_xnT(0)
            act.wait_ge(small_in, 48)
            xt_bias(0)
            v_hi(1, 1)
            softexp(0, 0, fresh=True)

            def block0_step(g, v, first=False, last=False):
                copy_xnT(g)
                softexp(2 * g - 1, 1, fresh=first)
                if not last:
                    v_hi(g + 1, v)
                xt_bias(g)
                softexp(2 * g, 0)
            block0_step(1, 0, first=True)
            with act.Fori(1, NB // 2 - 1) as m:
                for u in range(2):
                    block0_step(2 * m + u, 1 - u)
            block0_step(NB - 2, 1)
            block0_step(NB - 1, 0, last=True)
            softexp(NP - 1, 1)
            for u in range(2):
                softexp(NP + u, u)
            act.wait_ge(xt_lo, NB)
            drain(0)

            def keep_x1(b):
                act.wait_ge(ec, EC * b + 8 + TB)
                act.activation(bass.AP(xres, b * TB * D, [[NT * D, P], [D, TB], [1, D]]), accs[:, :, 0:D],
                               ACT.Copy).then_inc(x1_kept, 1)

            def attention(b, last=False):
                with act.Fori(1, 4) as h:
                    for u in range(2):
                        softexp(b * NP + 2 * h + u, u)
                keep_x1(b - 1)
                with act.Fori(4, NP // 2) as h:
                    for u in range(2):
                        softexp(b * NP + 2 * h + u, u)
                if not last:
                    for u in range(2):
                        softexp((b + 1) * NP + u, u)
                drain(b)

            with act.Fori(1, NB - 1) as b:
                attention(b)
            attention(NB - 1, last=True)

            def copy_hT(b):
                act.wait_ge(ht_ok, b + 1)
                act.activation(xnTh[:, b * BLK:(b + 1) * BLK], sc16[:, b % 2, 0, :], ACT.Copy).then_inc(ht_hi, 1)
                act.activation(xnTl[:, b * BLK:(b + 1) * BLK], sc16[:, b % 2, 1, :], ACT.Copy).then_inc(ht_lo, 1)
            for b in range(NB - 3):
                copy_hT(b)
                if b == 2:
                    keep_x1(NB - 1)
            act.wait_ge(lmax_ok, 1)
            act.activation(rt[:, 0, :], acc[:, 1, 0:E], ACT.Exp, bias=rc[:, 1:2]).then_inc(lexp_ok, 1)

            act.wait_ge(b1t_ok, 1)
            act.activation(b1cols[:, :], acc[:, 2, 0:E * FT], ACT.Copy).then_inc(b1c_ok, 1)
            for b in range(NB - 3, NB):
                copy_hT(b)

            def weights_hi(q):
                act.wait_ge(w1_in[q], 16)
                act.activation(w1h[:, q], w1f[:, q], ACT.Copy, scale=WSCALE).then_inc(w1_hi, 1)
                act.wait_ge(w2_sc, q + 1)
                act.activation(w2h[:, q], w2f[:, q], ACT.Copy).then_inc(w2_hi, 1)

            def gelus(q, u, n, fresh=False):
                act.wait_ge(up_ok, n + 1)
                if not fresh:
                    act.wait_ge(g_ok, n - 1)
                for s in range(2):
                    act.activation(ebuf[:, u, s * IB:(s + 1) * IB], sc[:, u, s, :], ACT.Gelu,
                                   bias=b1sel[:, 2 * q + s:2 * q + s + 1], scale=1.0 / WSCALE).then_inc(gelu_ok, 1)

            def ffn(b, last=False):
                for q in range(2, NQ):
                    gelus(q, q % 2, b * NQ + q)
                if not last:
                    for q in range(2):
                        gelus(q, q, (b + 1) * NQ + q)
                act.wait_ge(down_ok, NQ * (b + 1))
                act.wait_ge(fin_ok, b)
                for t in range(TB):
                    act.activation(accs[:, t, 0:D], acc[:, t, 0:D], ACT.Copy, scale=1.0 / WSCALE).then_inc(y_out, 1)

            for q in range(2):
                weights_hi(q)
            act.wait_ge(b1sel_ok, TOP)
            for q in range(NQ):
                if q + 2 < NQ:
                    weights_hi(q + 2)
                gelus(q, q % 2, q, fresh=(q < 2))
            for q in range(2):
                gelus(q, q, NQ + q)
            act.wait_ge(down_ok, NQ)
            for t in range(TB):
                act.activation(accs[:, t, 0:D], acc[:, t, 0:D], ACT.Copy, scale=1.0 / WSCALE).then_inc(y_out, 1)
            with act.Fori(1, NB - 1) as b:
                ffn(b)
            ffn(NB - 1, last=True)

        @block.vector
        def _(ve):
            ve.wait_ge(iota_ok, 1)
            ve.scalar_tensor_tensor(out=ltoe[:, 1, :], in0=ltoe[:, 0, :], scalar=-1.0, in1=ltoe[:, 0, :],
                                    op0=ALU.mult, op1=ALU.max).then_inc(lchain, 1)
            ve.wait_ge(lchain, 1)
            ve.tensor_scalar(ltoe[:, 2, :], ltoe[:, 1, :], EPS_W, None, ALU.add).then_inc(lchain, 1)
            ve.wait_ge(lchain, 2)
            ve.reciprocal(ltoe[:, 1, :], ltoe[:, 2, :]).then_inc(lchain, 1)
            ve.wait_ge(lchain, 3)
            ve.scalar_tensor_tensor(out=ltoe[:, 3, :], in0=ltoe[:, 0, :], scalar=0.0, in1=ltoe[:, 1, :],
                                    op0=ALU.not_equal, op1=ALU.mult).then_inc(ltoe_ok, 1)

            def norm_stats(src, n, u):
                if not isinstance(n, int) or n > 0:
                    ve.wait_ge(mv_ok, TB * n)
                ve.nop(nofuse=True)
                for t in range(TB):
                    ve.bn_stats(stats[:, u, t, :], src(t)).then_inc(st_ok, 1)
                ve.wait_ge(st_ok, TB * n + TB)
                ve.nop(nofuse=True)
                for t in range(TB):
                    ve.bn_aggr(mv[:, u, t, :], stats[:, u, t, :]).then_inc(mv_ok, 1)
                ve.wait_ge(mv_ok, TB * n + TB)

            def norm_var(n, u):
                ve.tensor_scalar(vtmp[:, u, :], mv[:, u, :, 1], EPS_LN, None, ALU.add).then_inc(var_ok, 1)

            def xtile(g):
                return lambda t: xres[:, TB * g + t, :]

            def xtile(g):
                return lambda t: bass.AP(xres, (TB * g + t) * D, [[NT * D, P], [1, D]])

            def x_stats(g, u):
                if not isinstance(g, int) or g >= 2:
                    ve.wait_ge(xn_ok, g - 1)
                norm_stats(xtile(g), g, u)
                norm_var(g, u)

            def x_norm(g, u):
                ve.wait_ge(rstd_ok, g + 1)
                if not isinstance(g, int) or g >= 2:
                    ve.wait_ge(vl_ok, g - 1)
                for t in range(TB):
                    ins = ve.tensor_scalar(xn_f[:, u, t, :], xtile(g)(t), mv[:, u, t, 0:1],
                                           rstd[:, u, t:t + 1], ALU.subtract, ALU.mult)
                ins.then_inc(xn_ok, 1)

            def xt_split(g):
                ve.wait_ge(xtf_ok, KD * (g + 1))
                hi = xtTh[:, bass.ds(g * BLK, BLK)]
                ve.tensor_copy(hi, xtf).then_inc(xt_hi, 1)
                ve.wait_ge(xt_hi, g + 1)
                ve.tensor_tensor(xtTl[:, bass.ds(g * BLK, BLK)], xtf, hi, ALU.subtract).then_inc(xt_lo, 1)

            def weigh(b, jp, u):
                ve.wait_ge(scores_ok, b * NP + jp + 1)
                ve.tensor_tensor(zbuf[:, u].rearrange("p (s c) -> p s c", s=2), sc[:, u], lwpair(b, jp),
                                 ALU.mult).then_inc(z_ok, 1)

            def split(n, u, fresh=False):
                ve.wait_ge(exp_ok, n + 1)
                if not fresh:
                    ve.wait_ge(pv_ok, n - 1)
                ve.tensor_copy(ph[:, u], ebuf[:, u]).then_inc(phi_ok, 1)
                ve.wait_ge(phi_ok, n + 1)
                ve.tensor_tensor(pl[:, u], ebuf[:, u], ph[:, u], ALU.subtract).then_inc(p_ok, 1)

            accd = accs[:, :, 0:D]

            def epi_diag_hi(b):
                ve.wait_ge(acc_out, TB * (b + 1))
                ve.tensor_scalar(den[:, :], accs[:, :, D], -1.0, EPS_W, ALU.add, ALU.add).then_inc(ec, 1)
                ve.tensor_tensor(accd, accd, vblock(b, 0, D), ALU.subtract).then_inc(ec, 1)

            def epi_diag_lo(b):
                ve.wait_ge(ec, EC * b + 2)
                ve.reciprocal(rden[:, :], den[:, :]).then_inc(ec, 1)
                ve.tensor_tensor(accd, accd, vblock(b, VLO, D), ALU.subtract).then_inc(ec, 1)

            def epi_att_stats(b):
                ve.wait_ge(ec, EC * b + 4)
                norm_stats(lambda t: accs[:, t, 0:D], NB + 2 * b, 0)

            def epi_att_var(b):
                ve.tensor_tensor(vsc[:, 0, :], mv[:, 0, :, 1], rden[:, :], ALU.mult).then_inc(ec, 1)
                ve.wait_ge(ec, EC * b + 5)
                ve.tensor_tensor(vsc[:, 1, :], vsc[:, 0, :], rden[:, :], ALU.mult).then_inc(ec, 1)
                ve.wait_ge(ec, EC * b + 6)
                ve.tensor_scalar(vtmp[:, 0, :], vsc[:, 1, :], EPS_LN, None, ALU.add).then_inc(var_ok, 1)

            def epi_att_norm(b):
                ve.wait_ge(rstd_ok, NB + 2 * b + 1)
                ve.tensor_tensor(kfac[:, :], rstd[:, 0, :], rden[:, :], ALU.mult).then_inc(ec, 1)
                ve.wait_ge(ec, EC * b + 7)
                for t in range(TB):
                    ve.tensor_scalar(accs[:, t, 0:D], accs[:, t, 0:D], mv[:, 0, t, 0:1], kfac[:, t:t + 1],
                                     ALU.subtract, ALU.mult).then_inc(ec, 1)

            def epi_x1(b):
                ve.wait_ge(ec, EC * b + 7 + TB)
                x = bass.AP(xres, b * TB * D, [[NT * D, P], [D, TB], [1, D]])
                ve.tensor_tensor(accd, x, accd, ALU.add).then_inc(ec, 1)

            def epi_x1_stats(b):
                ve.wait_ge(ec, EC * b + 8 + TB)
                norm_stats(lambda t: accs[:, t, 0:D], NB + 2 * b + 1, 1)
                norm_var(NB + 2 * b + 1, 1)

            def epi_h(b):
                ve.wait_ge(rstd_ok, NB + 2 * b + 2)
                ve.wait_ge(x1_kept, b + 1)
                for t in range(TB):
                    ve.tensor_scalar(accs[:, t, 0:D], accs[:, t, 0:D],
                                     mv[:, 1, t, 0:1], rstd[:, 1, t:t + 1], ALU.subtract, ALU.mult).then_inc(ec, 1)

            def epi_h_sum(b):
                ve.wait_ge(ec, EC * b + 8 + 2 * TB)
                ve.tensor_reduce(htot[:, :], accs[:, :, 0:D].rearrange("p t d -> p d t"), AX_X, ALU.add).then_inc(ec, 1)
                hh = bass.AP(xtTh, b * BLK, [[NB * BLK, P], [D, TB], [1, D]])
                ve.tensor_copy(hh, accd).then_inc(ec, 1)
                ve.wait_ge(ec, EC * b + 10 + 2 * TB)

            def epi_h_lo(b):
                ve.wait_ge(ec, EC * (b + 1))
                hh = bass.AP(xtTh, b * BLK, [[NB * BLK, P], [D, TB], [1, D]])
                hl = bass.AP(xtTl, b * BLK, [[NB * BLK, P], [D, TB], [1, D]])
                ve.tensor_tensor(hsum[:, :], hsum[:, :], htot[:, :], ALU.add).then_inc(hs_ok, 1)
                ve.tensor_tensor(hl, accd, hh, ALU.subtract).then_inc(epi_ok, 1)

            ve.wait_ge(x_in[0], 16)
            x_stats(0, 0)
            ve.wait_ge(w_in, 16)
            ve.wait_ge(w_hi, 1)
            ve.scalar_tensor_tensor(out=Wl[:, :, :], in0=Wf[:, :, :], scalar=WSCALE, in1=Wh[:, :, :],
                                    op0=ALU.mult, op1=ALU.subtract).then_inc(w_lo, 1)
            x_norm(0, 0)
            ve.wait_ge(x_in[1], 16)
            x_stats(1, 1)
            x_norm(1, 1)
            xt_split(0)
            ve.wait_ge(consts, 7)
            ve.wait_ge(lw_in[0], 16)
            weigh(0, 0, 0)
            weigh(0, 1, 1)
            split(0, 0, fresh=True)

            def block0_step(g, v, first=False, last=False):
                if not last:
                    x_stats(g + 1, v)
                weigh(0, 2 * g, 0)
                split(2 * g - 1, 1, fresh=first)
                if not last:
                    x_norm(g + 1, v)
                xt_split(g)
                weigh(0, 2 * g + 1, 1)
                split(2 * g, 0)
            ve.wait_ge(x_in[2], 16)
            block0_step(1, 0, first=True)
            ve.wait_ge(xrest_in, 16 * (NB - 3))
            ve.wait_ge(lw_in[1], 16)
            with ve.Fori(1, NB // 2 - 1) as m:
                for u in range(2):
                    block0_step(2 * m + u, 1 - u)
            block0_step(NB - 2, 1)
            block0_step(NB - 1, 0, last=True)
            ve.wait_ge(lw_in[2], 16)
            for jp in range(2):
                weigh(1, jp, jp)
                split(NP - 1 + jp, 1 - jp)

            def attention(b, last=False):
                for jp in range(2, 10):
                    weigh(b, jp, jp % 2)
                    split(b * NP + jp - 1, (jp - 1) % 2)
                    if jp == 2:
                        epi_diag_hi(b - 1)
                    if jp == 3:
                        epi_diag_lo(b - 1)
                    if jp == 4:
                        epi_att_stats(b - 1)
                        epi_att_var(b - 1)
                    if jp == 5:
                        epi_att_norm(b - 1)
                    if jp == 6:
                        epi_x1(b - 1)
                    if jp == 7:
                        epi_x1_stats(b - 1)
                    if jp == 8:
                        epi_h(b - 1)
                    if jp == 9:
                        epi_h_sum(b - 1)
                        epi_h_lo(b - 1)
                with ve.Fori(5, NP // 2) as h:
                    for u in range(2):
                        weigh(b, 2 * h + u, u)
                        split(b * NP + 2 * h + u - 1, 1 - u)
                for jp in range(2):
                    if not last:
                        weigh(b + 1, jp, jp)
                    if jp == 0 or not last:
                        split(b * NP + NP + jp - 1, 1 - jp)

            with ve.Fori(1, NB - 1) as b:
                attention(b)
            attention(NB - 1, last=True)
            epi_diag_hi(NB - 1)
            epi_diag_lo(NB - 1)
            epi_att_stats(NB - 1)
            epi_att_var(NB - 1)
            epi_att_norm(NB - 1)
            epi_x1(NB - 1)
            epi_x1_stats(NB - 1)
            epi_h(NB - 1)
            epi_h_sum(NB - 1)
            epi_h_lo(NB - 1)

            links = [0]

            def link(ins):
                links[0] += 1
                ins.then_inc(rchain, 1)
                ve.wait_ge(rchain, links[0])
            LMAX, NLMAX, ESUM, ERCP, P1, R1, P2, R2, PS, PR, C1, C2 = (rc[:, i:i + 1] for i in range(12))
            EXPS, PROBS, CAND1, ONE1, REST, CAND2, ONE2, COMB1 = (rt[:, i, :] for i in range(8))
            ve.wait_ge(hmean_ok, 1)
            link(ve.tensor_copy(meanT[:, :], acc[:, 0, 0:KD]))
            for k in range(KD):
                ve.tensor_scalar(meanB[:, k, :], ones[:, :], meanT[:, k:k + 1], None, ALU.mult).then_inc(meanT_ok, 1)
            ve.wait_ge(logit_ok, 1)
            link(ve.tensor_reduce(LMAX, acc[:, 1, 0:E], AX_X, ALU.max))
            ve.tensor_scalar(NLMAX, LMAX, -1.0, None, ALU.mult).then_inc(lmax_ok, 1)
            ve.wait_ge(lexp_ok, 1)
            link(ve.tensor_reduce(ESUM, EXPS, AX_X, ALU.add))
            link(ve.reciprocal(ERCP, ESUM))
            link(ve.tensor_scalar(PROBS, EXPS, ERCP, None, ALU.mult))
            link(ve.tensor_reduce(P1, PROBS, AX_X, ALU.max))
            link(ve.scalar_tensor_tensor(out=CAND1, in0=PROBS, scalar=P1, in1=rev[:, :],
                                         op0=ALU.is_equal, op1=ALU.mult))
            link(ve.tensor_reduce(R1, CAND1, AX_X, ALU.max))
            link(ve.tensor_scalar(ONE1, rev[:, :], R1, None, ALU.is_equal))
            link(ve.scalar_tensor_tensor(out=REST, in0=ONE1, scalar=-2.0, in1=PROBS, op0=ALU.mult, op1=ALU.add))
            link(ve.tensor_reduce(P2, REST, AX_X, ALU.max))
            link(ve.scalar_tensor_tensor(out=CAND2, in0=REST, scalar=P2, in1=rev[:, :],
                                         op0=ALU.is_equal, op1=ALU.mult))
            link(ve.tensor_reduce(R2, CAND2, AX_X, ALU.max))
            ve.tensor_scalar(eidx[:, 0:1], R1, -1.0, float(E), ALU.mult, ALU.add).then_inc(route_ok, 1)
            ve.tensor_scalar(eidx[:, 1:2], R2, -1.0, float(E), ALU.mult, ALU.add).then_inc(route_ok, 1)
            link(ve.tensor_scalar(ONE2, rev[:, :], R2, None, ALU.is_equal))
            link(ve.tensor_tensor(PS, P1, P2, ALU.add))
            link(ve.reciprocal(PR, PS))
            link(ve.tensor_tensor(C1, P1, PR, ALU.mult))
            link(ve.tensor_tensor(C2, P2, PR, ALU.mult))
            link(ve.tensor_scalar(COMB1, ONE1, C1, None, ALU.mult))
            link(ve.scalar_tensor_tensor(out=comb[:, :], in0=ONE2, scalar=C2, in1=COMB1, op0=ALU.mult, op1=ALU.add))
            ve.wait_ge(b1c_ok, 1)
            for i, one in enumerate((ONE1, ONE2)):
                link(ve.tensor_tensor(bprod[:, i], b1cols[:, :].rearrange("p (e t) -> p t e", e=E),
                                      one.unsqueeze(1).broadcast_to([P, FT, E]), ALU.mult))
                ve.tensor_reduce(b1sel[:, i * FT:(i + 1) * FT], bprod[:, i], AX_X, ALU.add).then_inc(b1sel_ok, 1)

            def w2_scale(q):
                ve.wait_ge(w2_in[q], 16)
                ve.tensor_scalar(w2f[:, q], w2f[:, q], (C1, C2)[q // FP], WSCALE, ALU.mult, ALU.mult).then_inc(w2_sc, 1)

            def weights_lo(q):
                ve.wait_ge(w1_hi, q + 1)
                ve.scalar_tensor_tensor(out=w1l[:, q], in0=w1f[:, q], scalar=WSCALE, in1=w1h[:, q],
                                        op0=ALU.mult, op1=ALU.subtract).then_inc(w1_lo, 1)
                ve.wait_ge(w2_hi, q + 1)
                ve.tensor_tensor(w2l[:, q], w2f[:, q], w2h[:, q], ALU.subtract).then_inc(w2_lo, 1)

            def gsplit(n, u, fresh=False):
                ve.wait_ge(gelu_ok, 2 * n + 2)
                if not fresh:
                    ve.wait_ge(down_ok, n - 1)
                ve.tensor_copy(ph[:, u], ebuf[:, u]).then_inc(ghi_ok, 1)
                ve.wait_ge(ghi_ok, n + 1)
                ve.tensor_tensor(pl[:, u], ebuf[:, u], ph[:, u], ALU.subtract).then_inc(g_ok, 1)

            def fin_bias(b):
                ve.wait_ge(y_out, TB * (b + 1))
                ve.tensor_tensor(accd, accd, b2c[:, :].unsqueeze(1).broadcast_to([P, TB, D]), ALU.add).then_inc(fc, 1)

            def fin_stats(b):
                ve.wait_ge(fc, (TB + 1) * b + 1)
                norm_stats(lambda t: accs[:, t, 0:D], 3 * NB + b, 0)
                norm_var(3 * NB + b, 0)

            def fin_norm(b):
                ve.wait_ge(rstd_ok, 3 * NB + b + 1)
                for t in range(TB):
                    ve.tensor_scalar(accs[:, t, 0:D], accs[:, t, 0:D], mv[:, 0, t, 0:1], rstd[:, 0, t:t + 1],
                                     ALU.subtract, ALU.mult).then_inc(fc, 1)

            def fin_add(b):
                ve.wait_ge(fc, (TB + 1) * (b + 1))
                x2 = bass.AP(xres, b * TB * D, [[NT * D, P], [D, TB], [1, D]])
                ve.tensor_tensor(x2, x2, accd, ALU.add).then_inc(fin_ok, 1)

            for q in range(2):
                w2_scale(q)
            for q in range(2):
                weights_lo(q)
            for q in range(NQ):
                if q + 2 < NQ:
                    w2_scale(q + 2)
                    weights_lo(q + 2)
                gsplit(q, q % 2, fresh=(q < 2))
                if q == 3:
                    ve.wait_ge(b2_in, 16)
                    link(ve.tensor_scalar(b2c[:, :], b2all[:, 0, :], comb[:, 0:1], None, ALU.mult))
                if q >= 4 and q < 4 + (E - 1 + 1) // 2:
                    for e in range(1 + 2 * (q - 4), min(3 + 2 * (q - 4), E)):
                        link(ve.scalar_tensor_tensor(out=b2c[:, :], in0=b2all[:, e, :], scalar=comb[:, e:e + 1],
                                                     in1=b2c[:, :], op0=ALU.mult, op1=ALU.add))

            def ffn(b):
                for q in range(NQ):
                    gsplit(b * NQ + q, q % 2)
                    if q == 2:
                        fin_bias(b - 1)
                    if q == 3:
                        fin_stats(b - 1)
                    if q == 4:
                        fin_norm(b - 1)
                    if q == 5:
                        fin_add(b - 1)
            with ve.Fori(1, NB) as b:
                ffn(b)
            fin_bias(NB - 1)
            fin_stats(NB - 1)
            fin_norm(NB - 1)
            fin_add(NB - 1)


_INS = ['L0_attn_x', 'L0_attn_W', 'L0_attn_b', 'L0_ffn_gate_w', 'L0_ffn_w1', 'L0_ffn_b1', 'L0_ffn_w2', 'L0_ffn_b2']
_OUTS = [((1, 4096, 256), 'float32')]


def kernel(**inputs):
    import numpy as _np
    import concourse.bacc as _bacc
    from concourse import mybir as _mybir
    from concourse.bass_utils import run_bass_kernel_spmd as _run

    nc = _bacc.Bacc("TRN2", target_bir_lowering=False, num_devices=1)
    arrays, args = {}, []
    for name in _INS:
        a = _np.ascontiguousarray(inputs[name])
        arrays[f"in_{name}_dram"] = a
        args.append(nc.dram_tensor(f"in_{name}_dram", a.shape, _mybir.dt.from_np(a.dtype), kind="ExternalInput").ap())
    for i, (shape, dtype) in enumerate(_OUTS):
        dt = _mybir.dt.from_np(_np.dtype(dtype))
        args.append(nc.dram_tensor(f"out_{i}_dram", shape, dt, kind="ExternalOutput").ap())
    program(nc, *args)
    r = _run(nc, [arrays], core_ids=[0])
    return r.results[0]["out_0_dram"]
```

```python
from contextlib import ExitStack

import concourse.bass as bass
from concourse import mybir

ALU = mybir.AluOpType
ACT = mybir.ActivationFunctionType
AX_X = mybir.AxisListType.X
F32 = mybir.dt.float32
F16 = mybir.dt.float16
I32 = mybir.dt.int32

P = 128
EPS_LN = 1e-5
EPS_W = 1e-7
WSCALE = 16.0
TOP = 2
WARM = 64


def program(nc, x_d, W_d, b_d, gate_d, w1_d, b1_d, w2_d, b2_d, out_d):
    _, S, D = x_d.shape
    E, _, F = w1_d.shape
    KD = D // P
    NT = S // P
    IB = 512
    TB = IB // P
    NB = S // IB
    NP = NT // 2
    BLK = KD * IB
    VW = 2 * D + 2
    VLO = D + 2
    LWOFF = S - 1
    LWW = 2 * S - P
    LW0 = LWOFF - (IB - 1)
    LWCUT = (LW0, LW0 + LWW // 4, LWW)
    LC = 2 * S // P
    FT = F // P
    FP = FT // 2
    NQ = TOP * FP
    FC = 2 * P
    LWA = max(LWW, NQ * (KD * FC + 2 * D))
    PF = 3 * NB + 2
    EC = 9 + 2 * TB

    with ExitStack() as ctx:
        def sb(name, shape, dt=F32):
            return ctx.enter_context(nc.sbuf_tensor(name, shape, dt))

        def sem(name):
            return ctx.enter_context(nc.semaphore(name))

        xres = sb("xres", [P, NT, D])
        lw = sb("lw", [P, LWA])
        vmat = sb("vmat", [P, NT * VW], F16)
        xnTh = sb("xnTh", [P, NB * BLK], F16)
        xnTl = sb("xnTl", [P, NB * BLK], F16)
        xtTh = sb("xtTh", [P, NB * BLK], F16)
        xtTl = sb("xtTl", [P, NB * BLK], F16)
        zbuf = sb("zbuf", [P, 2, 2 * IB])
        ebuf = sb("ebuf", [P, 2, 2 * IB])
        ph = sb("ph", [P, 2, 2 * IB], F16)
        pl = sb("pl", [P, 2, 2 * IB], F16)
        accs = sb("accs", [P, TB, D + 1])
        hsum = sb("hsum", [P, D])
        bprod = sb("bprod", [P, TOP, FT, E])
        ltoe = sb("ltoe", [P, 4, LC])
        xn_f = sb("xn_f", [P, 2, TB, D])
        Wh = sb("Wh", [P, KD, D], F16)
        Wl = sb("Wl", [P, KD, D], F16)
        bcol = sb("bcol", [P, KD])
        gate = sb("gate", [P, KD, E])
        b1rows = sb("b1rows", [E * FT, P])
        b1cols = sb("b1cols", [P, E * FT])
        b1sel = sb("b1sel", [P, TOP * FT])
        ident = sb("ident", [P, P], F16)
        identf = sb("identf", [P, P])
        ones = sb("ones", [P, P])
        tcol = sb("tcol", [P, 1])
        half = sb("half", [P, 2 * TB])
        stats = sb("stats", [P, 2, TB, 6])
        mv = sb("mv", [P, 2, TB, 2])
        rstd = sb("rstd", [P, 2, TB])
        rden = sb("rden", [P, TB])
        den = sb("den", [P, TB])
        rden2 = sb("rden2", [P, TB])
        mk = sb("mk", [P, TB])
        kfac = sb("kfac", [P, TB])
        vsc = sb("vsc", [P, TB])
        htot = sb("htot", [P, D])
        vtmp = sb("vtmp", [P, 2, TB])
        meanT = sb("meanT", [P, KD])
        meanB = sb("meanB", [P, KD, P])
        rt = sb("rt", [P, 12, E])
        rc = sb("rc", [P, 16])
        rev = sb("rev", [P, E])
        eidx = sb("eidx", [P, TOP], I32)
        comb = sb("comb", [P, E])
        b2c = sb("b2c", [P, D])

        Wf = zbuf[:, 0, 0:KD * D].rearrange("p (k n) -> p k n", k=KD)
        xtf = accs[:, :, :].rearrange("p t w -> p (t w)")[:, 0:BLK]
        xdiag = xn_f[:, 0]
        b2all = xn_f[:, :, :, :].rearrange("p u t d -> p (u t) d")
        w1f = lw[:, 0:NQ * KD * FC].rearrange("p (q k f) -> p q k f", q=NQ, k=KD)
        w2f = lw[:, NQ * KD * FC:NQ * KD * FC + NQ * 2 * D].rearrange("p (q s d) -> p q s d", q=NQ, s=2)
        n_w = NQ * KD * FC

        def wview(n):
            return vmat[:, n * n_w:(n + 1) * n_w].rearrange("p (q k f) -> p q k f", q=NQ, k=2)
        w1h, w1l, w2h, w2l = (wview(n) for n in range(4))

        sc = ctx.enter_context(nc.psum_tensor("sc", [P, 2, 2, IB], F32))
        acc = ctx.enter_context(nc.psum_tensor("acc", [P, TB, 512], F32))

        x_in = [sem(f"x_in{g}") for g in range(4)]
        xrest_in = sem("xrest_in")
        w_in = sem("w_in")
        small_in = sem("small_in")
        b2_in = sem("b2_in")
        lchain = sem("lchain")
        ltoe_ok = sem("ltoe_ok")
        lflat_out = sem("lflat_out")
        lw_in = [sem(f"lw_in{c}") for c in range(3)]
        consts = sem("consts")
        ident_ok = sem("ident_ok")
        iota_ok = sem("iota_ok")
        ones_col = sem("ones_col")
        st_ok = sem("st_ok")
        mv_ok = sem("mv_ok")
        xtf_ok = sem("xtf_ok")
        ec = sem("ec")
        xdiag_ok = sem("xdiag_ok")
        x1_kept = sem("x1_kept")
        hs_ok = sem("hs_ok")
        rchain = sem("rchain")
        fc = sem("fc")
        var_ok = sem("var_ok")
        rstd_ok = sem("rstd_ok")
        xn_ok = sem("xn_ok")
        vh_ok = sem("vh_ok")
        vl_ok = sem("vl_ok")
        w_hi = sem("w_hi")
        w_lo = sem("w_lo")
        tp_ok = sem("tp_ok")
        tp_hi = sem("tp_hi")
        tp_lo = sem("tp_lo")
        xt_ok = sem("xt_ok")
        xt_hi = sem("xt_hi")
        xt_lo = sem("xt_lo")
        scores_ok = sem("scores_ok")
        z_ok = sem("z_ok")
        tanh_ok = sem("tanh_ok")
        exp_ok = sem("exp_ok")
        phi_ok = sem("phi_ok")
        p_ok = sem("p_ok")
        pv_ok = sem("pv_ok")
        acc_done = sem("acc_done")
        acc_out = sem("acc_out")
        epi_ok = sem("epi_ok")
        b1t_ok = sem("b1t_ok")
        b1c_ok = sem("b1c_ok")
        hmean_ok = sem("hmean_ok")
        meanT_ok = sem("meanT_ok")
        logit_ok = sem("logit_ok")
        lmax_ok = sem("lmax_ok")
        lexp_ok = sem("lexp_ok")
        route_ok = sem("route_ok")
        w1_in = [sem(f"w1_in{q}") for q in range(NQ)]
        w2_in = [sem(f"w2_in{q}") for q in range(NQ)]
        b1sel_ok = sem("b1sel_ok")
        w1_hi = sem("w1_hi")
        w1_lo = sem("w1_lo")
        w2_sc = sem("w2_sc")
        w2_hi = sem("w2_hi")
        w2_lo = sem("w2_lo")
        table_ok = sem("table_ok")
        ht_ok = sem("ht_ok")
        ht_hi = sem("ht_hi")
        ht_lo = sem("ht_lo")
        up_ok = sem("up_ok")
        gelu_ok = sem("gelu_ok")
        ghi_ok = sem("ghi_ok")
        g_ok = sem("g_ok")
        down_ok = sem("down_ok")
        last_down = sem("last_down")
        lastb = sem("lastb")
        tail = sem("tail")
        y_out = sem("y_out")
        fin_ok = sem("fin_ok")
        store_ok = sem("store_ok")

        def vtile(t, lo, n):
            base = t * VW + lo
            return vmat[:, base:base + n] if isinstance(t, int) else vmat[:, bass.ds(base, n)]

        def vblock(g, lo, n):
            return bass.AP(vmat, g * TB * VW + lo, [[NT * VW, P], [VW, TB], [1, n]])

        def tr(buf, g, k, c, n):
            return buf[:, bass.ds(g * BLK + k * IB + c, n)]

        def tdst(g, part):
            return acc16[:, (3, 0)[part], :] if isinstance(g, int) and g == 1 else sc16[:, 0, part, :]

        def lwpair(b, jp):
            return bass.AP(lw, b * -IB + jp * (2 * P) + LW0, [[LWA, P], [P, 2], [1, IB]])

        sc16 = sc[:, :, :, :].bitcast(F16)
        acc16 = acc[:, :, :].bitcast(F16)
        halves = (slice(0, TB // 2), slice(TB // 2, TB))

        lflat = nc.dram_tensor("lflat", [1, 2 * S], F32, kind="Internal").ap()

        block = ctx.enter_context(nc.Block())

        @block.sync
        def _(sp):
            xv = x_d[0].rearrange("(g t p) d -> g p t d", t=TB, p=P)
            def load_x(g, landed):
                sp.dma_start(xres[:, TB * g:TB * g + TB, :], xv[g]).then_inc(landed, 16)

            def load_lw(part, c0, c1):
                sp.dma_start(lw[:, c0:c1], bass.AP(lflat.tensor, c0, [[1, P], [1, c1 - c0]])).then_inc(lw_in[part], 16)

            load_x(0, x_in[0])
            sp.dma_start(Wf[:, :, :], W_d.rearrange("(k p) n -> p k n", p=P)).then_inc(w_in, 16)
            load_x(1, x_in[1])
            sp.wait_ge(ltoe_ok, 1)
            sp.dma_start(lflat.rearrange("a (p c) -> (a p) c", p=P), ltoe[:, 3, :]).then_inc(lflat_out, 16)
            load_x(2, x_in[2])
            sp.wait_ge(lflat_out, 16)
            load_lw(0, LWCUT[0], LWCUT[1])
            load_x(3, x_in[3])
            for g in range(4, NB):
                load_x(g, xrest_in)
            load_lw(1, LWCUT[1], LWCUT[2])
            load_lw(2, 0, LWCUT[0])

            for e in range(TOP):
                sp.wait_ge(route_ok, e + 1)
                ex = sp.value_load(eidx[0:1, e:e + 1], min_val=0, max_val=E - 1)
                for f in range(FP):
                    q = e * FP + f
                    sp.dma_start(w1f[:, q], w1_d[bass.ds(ex, 1), :, f * FC:(f + 1) * FC]
                                 .rearrange("a (k p) f -> p (a k) f", p=P)).then_inc(w1_in[q], 16)
                    sp.dma_start(w2f[:, q], w2_d[bass.ds(ex, 1), f * FC:(f + 1) * FC, :]
                                 .rearrange("a (s p) d -> p (a s) d", p=P)).then_inc(w2_in[q], 16)
            sp.dma_start(b2all, bass.AP(b2_d.tensor, 0, [[0, P], [D, E], [1, D]])).then_inc(b2_in, 16)
            ov = out_d[0].rearrange("(g t p) d -> g p t d", t=TB, p=P)
            for g in range(NB - 1):
                sp.wait_ge(fin_ok, g + 1)
                sp.dma_start(ov[g], xres[:, TB * g:TB * g + TB, :]).then_inc(store_ok, 16)
            for i, ts in enumerate(halves):
                sp.wait_ge(fin_ok, NB + i)
                sp.dma_start(ov[NB - 1][:, ts, :], xres[:, NT - TB + ts.start:NT - TB + ts.stop, :]).then_inc(store_ok, 16)
            sp.wait_ge(store_ok, 16 * (NB + 1))

        @block.gpsimd
        def _(pool):
            pool.iota(ltoe[:, 0, :], [[1, LC]], base=-LWOFF, channel_multiplier=LC,
                      allow_small_or_imprecise_dtypes=True).then_inc(iota_ok, 1)
            pool.memset(half[:, :], -0.5).then_inc(consts, 1)
            pool.memset(ident[:, :], 0.0).then_inc(consts, 1)
            pool.memset(identf[:, :], 0.0).then_inc(consts, 1)
            pool.wait_ge(consts, 3)
            for m in (ident, identf):
                pool.affine_select(out=m[:, :], in_=m[:, :], compare_op=ALU.not_equal, fill=1.0, base=0,
                                   pattern=[[-1, P]], channel_multiplier=1).then_inc(ident_ok, 1)
            pool.memset(vmat[:, :].rearrange("p (t w) -> p t w", w=VW)[:, :, D:D + 2], 1.0).then_inc(ones_col, 1)
            pool.memset(ones[:, :], 1.0).then_inc(consts, 1)
            pool.memset(tcol[:, :], 1.0 / S).then_inc(consts, 1)
            pool.memset(hsum[:, :], 0.0).then_inc(consts, 1)
            pool.memset(mk[:, :], 0.0).then_inc(x1_kept, 1)
            pool.iota(rev[:, :], [[-1, E]], base=E, channel_multiplier=0,
                      allow_small_or_imprecise_dtypes=True).then_inc(consts, 1)

            def power(n, u):
                pool.wait_ge(var_ok, n + 1)
                pool.tensor_tensor(rstd[:, u, :], vtmp[:, u, :], half[:, 0:TB], ALU.pow).then_inc(rstd_ok, 1)

            def ln_x(g, u):
                power(g, u)
                pool.wait_ge(vh_ok, g + 1)
                pool.tensor_tensor(vblock(g, VLO, D), xn_f[:, u], vblock(g, 0, D),
                                   ALU.subtract).then_inc(vl_ok, 1)
            for u in range(2):
                power(u, u)
            with pool.Fori(1, NB // 2) as m:
                for u in range(2):
                    ln_x(2 * m + u, u)
            pool.wait_ge(vh_ok, NB)
            def rebuild_xn(b):
                pool.wait_ge(vl_ok, NB)
                pool.tensor_tensor(xdiag, vblock(b, 0, D), vblock(b, VLO, D), ALU.add).then_inc(xdiag_ok, 1)

            def finish_x1(b):
                x1 = bass.AP(xres, b * TB * D, [[NT * D, P], [D, TB], [1, D]])
                pool.tensor_tensor(x1, x1, bass.AP(mk, 0, [[TB, P], [1, TB], [0, D]]), ALU.subtract).then_inc(x1_kept, 1)

            def part_power(n, u, ts):
                pool.wait_ge(var_ok, n + 1)
                pool.tensor_tensor(rstd[:, u, ts], vtmp[:, u, ts], half[:, ts], ALU.pow).then_inc(rstd_ok, 1)

            with pool.Fori(0, NB - 1) as b:
                rebuild_xn(b)
                for u in range(2):
                    power(NB + 2 * b + u, u)
                pool.wait_ge(ec, EC * b + 7 + 2 * TB)
                finish_x1(b)
            rebuild_xn(NB - 1)
            for u in range(2):
                for i, ts in enumerate(halves):
                    part_power(3 * NB - 2 + 2 * u + i, u, ts)
            pool.wait_ge(hs_ok, NB)
            finish_x1(NB - 1)
            with pool.Fori(0, NB - 1) as b:
                power(PF + b, 0)
            for i, ts in enumerate(halves):
                part_power(PF + NB - 1 + i, 0, ts)

        @block.tensor
        def _(pe):
            def transposes(g):
                if not isinstance(g, int) or g > 1:
                    pe.wait_ge(z_ok, 2 * g - 1)
                for part, lo in enumerate((0, VLO)):
                    dst = tdst(g, part)
                    pe.wait_ge((vh_ok, vl_ok)[part], g + 1)
                    for k in range(KD):
                        for t in range(TB):
                            mm = pe.transpose(dst[:, k * IB + t * P:k * IB + t * P + P],
                                              vtile(TB * g + t, lo + k * P, P), ident[:, :])
                    mm.then_inc(tp_ok, 1)

            def xt_product(g):
                pe.wait_ge(tp_hi, g + 1)
                if not isinstance(g, int) or g > 0:
                    pe.wait_ge(z_ok, 2 * g)
                for m in range(KD):
                    for i, (wp, xp) in enumerate(((Wh, xnTh), (Wl, xnTh), (Wh, xnTl))):
                        if m == 0 and i == 2:
                            pe.wait_ge(tp_lo, g + 1)
                        for k in range(KD):
                            mm = pe.matmul(sc[:, 1, m, :], wp[:, k, m * P:(m + 1) * P], tr(xp, g, k, 0, IB),
                                           start=(i == 0 and k == 0), stop=(i == 2 and k == KD - 1))
                    mm.then_inc(xt_ok, 1)

            def scores(b, h, u, wait_z=True, first=False):
                if wait_z:
                    pe.wait_ge(z_ok, b * NP + 2 * h + u - 1)
                for s in range(2):
                    for i, (jm, im) in enumerate(((xnTh, xtTh), (xnTl, xtTh), (xnTh, xtTl))):
                        if first and s == 0 and i == 2:
                            pe.wait_ge(xt_lo, KD)
                        for k in range(KD):
                            mm = pe.matmul(sc[:, u, s, :], tr(jm, h, k, (2 * u + s) * P, P), tr(im, b, k, 0, IB),
                                           start=(i == 0 and k == 0), stop=(i == 2 and k == KD - 1))
                mm.then_inc(scores_ok, 1)

            def pv(b, jp, u, start=False, stop=False, fresh=False):
                pe.wait_ge(p_ok, b * NP + jp + 1)
                for t in range(TB):
                    if start and not fresh:
                        pe.wait_ge(acc_out, TB * (b - 1) + t + 1)
                    for s in range(2):
                        jt = 2 * jp + s
                        pe.matmul(acc[:, t, 0:D + 1], ph[:, u, s * IB + t * P:s * IB + (t + 1) * P], vtile(jt, 0, D + 1),
                                  start=(start and s == 0), stop=False)
                        pe.matmul(acc[:, t, 0:D], ph[:, u, s * IB + t * P:s * IB + (t + 1) * P], vtile(jt, VLO, D),
                                  start=False, stop=False)
                        mm = pe.matmul(acc[:, t, 0:D + 1], pl[:, u, s * IB + t * P:s * IB + (t + 1) * P], vtile(jt, 0, D + 1),
                                       start=False, stop=(stop and s == 1))
                    if stop and t < TB - 1:
                        mm.then_inc(acc_done, 1)
                mm.then_inc(pv_ok, 1)

            def block0_step(g, first=False):
                if first:
                    pe.wait_ge(z_ok, 1)
                else:
                    transposes(g)
                    pv(0, 2 * g - 3, 1)
                pe.wait_ge(tp_hi, g + 1)
                pe.wait_ge(tp_lo, g + 1)
                scores(0, g, 0, wait_z=False)
                xt_product(g)
                pv(0, 2 * g - 2, 0, start=first, fresh=first)
                pe.wait_ge(xtf_ok, KD * (g + 1))
                scores(0, g, 1, wait_z=False)

            def warm_up(n, bank):
                with pe.Fori(0, n // 8):
                    for _ in range(8):
                        pe.transpose(acc16[:, bank, 0:P], ident[:, :], ident[:, :])

            pe.wait_ge(ident_ok, 2)
            warm_up(WARM, 3)
            pe.wait_ge(ones_col, 1)
            transposes(0)
            pe.wait_ge(w_hi, 1)
            pe.wait_ge(w_lo, 1)
            xt_product(0)
            pe.wait_ge(xt_hi, KD)
            scores(0, 0, 0, wait_z=False, first=True)
            transposes(1)
            scores(0, 0, 1, wait_z=False)
            block0_step(1, first=True)
            with pe.Fori(2, NB) as g:
                block0_step(g)
            pv(0, NP - 3, 1)
            pe.wait_ge(xt_hi, KD * NB)
            pe.wait_ge(xt_lo, KD * NB)
            for u in range(2):
                scores(1, 0, u)
                pv(0, NP - 2 + u, u, stop=(u == 1))

            def attention(b, last=False):
                for u in range(2):
                    scores(b, 1, u)
                    pv(b, u, u, start=(u == 0))
                with pe.Fori(1, NP // 2 - 1) as h:
                    for u in range(2):
                        scores(b, h + 1, u)
                        pv(b, 2 * h + u, u)
                for u in range(2):
                    if not last:
                        scores(b + 1, 0, u)
                    pv(b, NP - 2 + u, u, stop=(u == 1))

            with pe.Fori(1, NB - 1) as b:
                attention(b)
            attention(NB - 1, last=True)

            def h_transposes(b):
                pe.wait_ge(epi_ok, b + 1)
                if 2 <= b < NB - 1:
                    pe.wait_ge(ht_hi, b - 1)
                    pe.wait_ge(ht_lo, b - 1)
                for part, src in enumerate((xtTh, xtTl)):
                    dst = sc16[:, b % 2, part, :] if b < NB - 1 else acc16[:, (3, 0)[part], :]
                    for k in range(KD):
                        for t in range(TB):
                            at = b * BLK + t * D + k * P
                            mm = pe.transpose(dst[:, k * IB + t * P:k * IB + t * P + P],
                                              src[:, at:at + P], ident[:, :])
                mm.then_inc(ht_ok, 1)
            pe.wait_ge(z_ok, NB * NP)
            for b in range(NB - 1):
                h_transposes(b)

            pe.wait_ge(consts, 7)
            pe.wait_ge(small_in, 48)
            pe.wait_ge(hs_ok, NB)
            pe.wait_ge(acc_out, NT)
            for k in range(KD):
                mm = pe.matmul(acc[:, 0, k:k + 1], hsum[:, k * P:(k + 1) * P], tcol[:, :], start=True, stop=True)
            mm.then_inc(hmean_ok, 1)
            pe.wait_ge(meanT_ok, KD)
            for k in range(KD):
                mm = pe.matmul(acc[:, 1, 0:E], meanB[:, k, :], gate[:, k, :], start=(k == 0), stop=(k == KD - 1))
            mm.then_inc(logit_ok, 1)
            pe.transpose(acc[:, 2, 0:E * FT], b1rows[:, :], identf[0:E * FT, 0:E * FT]).then_inc(b1t_ok, 1)
            warm_up(WARM, 3)
            h_transposes(NB - 1)
            warm_up(WARM // 8 * 3, 1)

            def up(b, q, u, n, loaded=False, first=False):
                if not first:
                    pe.wait_ge(gelu_ok, 2 * n - 2)
                if not loaded:
                    pe.wait_ge(w1_hi, q + 1)
                    pe.wait_ge(w1_lo, q + 1)
                for s in range(2):
                    for i, (wm, hm) in enumerate(((w1h, xnTh), (w1l, xnTh), (w1h, xnTl))):
                        for k in range(KD):
                            mm = pe.matmul(sc[:, u, s, :], wm[:, q, k, s * P:(s + 1) * P], tr(hm, b, k, 0, IB),
                                           start=(i == 0 and k == 0), stop=(i == 2 and k == KD - 1))
                mm.then_inc(up_ok, 1)

            def down(b, q, u, n, loaded=False, fresh=False):
                pe.wait_ge(g_ok, n + 1)
                if not loaded:
                    pe.wait_ge(w2_hi, q + 1)
                    pe.wait_ge(w2_lo, q + 1)
                for t in range(TB):
                    if q == 0 and not fresh:
                        pe.wait_ge(y_out, TB * (b - 1) + t + 1)
                    for s in range(2):
                        c = s * IB + t * P
                        pe.matmul(acc[:, t, 0:D], ph[:, u, c:c + P], w2h[:, q, s, :],
                                  start=(q == 0 and s == 0), stop=False)
                        pe.matmul(acc[:, t, 0:D], ph[:, u, c:c + P], w2l[:, q, s, :], start=False, stop=False)
                        mm = pe.matmul(acc[:, t, 0:D], pl[:, u, c:c + P], w2h[:, q, s, :],
                                       start=False, stop=(q == NQ - 1 and s == 1))
                mm.then_inc(down_ok, 1)

            def last_downs(b, n):
                waited = 0
                for u, t in [(0, t) for t in range(TB - 1)] + [(1, t) for t in range(TB - 1)] + [(0, TB - 1), (1, TB - 1)]:
                    if u == waited:
                        pe.wait_ge(g_ok, n + u + 1)
                        waited += 1
                    for s in range(2):
                        c = s * IB + t * P
                        pe.matmul(acc[:, t, 0:D], ph[:, u, c:c + P], w2h[:, NQ - 2 + u, s, :], start=False, stop=False)
                        pe.matmul(acc[:, t, 0:D], ph[:, u, c:c + P], w2l[:, NQ - 2 + u, s, :], start=False, stop=False)
                        mm = pe.matmul(acc[:, t, 0:D], pl[:, u, c:c + P], w2h[:, NQ - 2 + u, s, :],
                                       start=False, stop=(u == 1 and s == 1))
                    if u == 1:
                        mm.then_inc(last_down, 1)

            def ffn(b, first=False, last=False):
                for q in range(NQ):
                    n = b * NQ + q
                    if q + 2 < NQ:
                        up(b, q + 2, q % 2, n + 2, loaded=not first)
                    elif not last:
                        up(b + 1, q + 2 - NQ, q % 2, n + 2, loaded=True)
                    if last and q >= NQ - 2:
                        continue
                    down(b, q, q % 2, n, loaded=not first, fresh=first)
                if last:
                    last_downs(b, b * NQ + NQ - 2)

            pe.wait_ge(ht_hi, NB - 1)
            pe.wait_ge(ht_lo, NB - 1)
            for q in range(2):
                up(0, q, q, q, first=True)
            pe.wait_ge(ht_hi, NB)
            pe.wait_ge(ht_lo, NB)
            ffn(0, first=True)
            with pe.Fori(1, NB - 1) as b:
                ffn(b)
            ffn(NB - 1, last=True)

        @block.scalar
        def _(act):
            act.dma_start(gate[:, :, :], gate_d.rearrange("(k p) e -> p k e", p=P)).then_inc(small_in, 16)
            act.dma_start(bcol[:, :], b_d.rearrange("(k p) -> p k", p=P), allow_slow_non_contiguous=True).then_inc(small_in, 16)
            act.dma_start(b1rows[:, :], b1_d.rearrange("e (t p) -> (e t) p", p=P)).then_inc(small_in, 16)
            act.wait_ge(w_in, 16)
            act.activation(Wh[:, :, :], Wf[:, :, :], ACT.Copy, scale=WSCALE).then_inc(w_hi, 1)

            def v_hi(g, u):
                act.wait_ge(xn_ok, g + 1)
                act.activation(vblock(g, 0, D), xn_f[:, u], ACT.Copy).then_inc(vh_ok, 1)

            def copy_xnT(g):
                act.wait_ge(tp_ok, 2 * g + 1)
                act.activation(xnTh[:, bass.ds(g * BLK, BLK)], tdst(g, 0), ACT.Copy).then_inc(tp_hi, 1)
                act.wait_ge(tp_ok, 2 * g + 2)
                act.activation(xnTl[:, bass.ds(g * BLK, BLK)], tdst(g, 1), ACT.Copy).then_inc(tp_lo, 1)

            def xt_bias(g):
                if not isinstance(g, int) or g > 0:
                    act.wait_ge(xt_lo, KD * g)
                for m in range(KD):
                    act.wait_ge(xt_ok, KD * g + m + 1)
                    act.activation(bass.AP(accs, m * IB + IB - 1, [[TB * (D + 1), P], [-1, IB]]), sc[:, 1, m, :], ACT.Identity,
                                   bias=bcol[:, m:m + 1], scale=1.0 / WSCALE).then_inc(xtf_ok, 1)

            def softexp(n, u, fresh=False):
                act.wait_ge(z_ok, n + 1)
                act.activation(zbuf[:, u], zbuf[:, u], ACT.Tanh).then_inc(tanh_ok, 1)
                act.wait_ge(tanh_ok, n + 1)
                if not fresh:
                    act.wait_ge(p_ok, n - 1)
                act.activation(bass.AP(ebuf, u * 2 * IB + IB - 1, [[4 * IB, P], [IB, 2], [-1, IB]]),
                               zbuf[:, u].rearrange("p (s c) -> p s c", s=2), ACT.Exp).then_inc(exp_ok, 1)

            def drain(b):
                if not isinstance(b, int) or b > 0:
                    act.wait_ge(epi_ok, b)
                for t in range(TB):
                    if t < TB - 1:
                        act.wait_ge(acc_done, (TB - 1) * b + t + 1)
                    else:
                        act.wait_ge(pv_ok, NP * (b + 1))
                    act.activation(accs[:, t, :], acc[:, t, 0:D + 1], ACT.Copy).then_inc(acc_out, 1)

            copy_xnT(0)
            act.wait_ge(small_in, 48)
            xt_bias(0)
            v_hi(1, 1)

            def block0_step(g, v, first=False, last=False):
                copy_xnT(g)
                if first:
                    softexp(0, 0, fresh=True)
                softexp(2 * g - 1, 1, fresh=first)
                if first:
                    xt_bias(g)
                if not last:
                    v_hi(g + 1, v)
                if not first:
                    xt_bias(g)
                softexp(2 * g, 0)
            block0_step(1, 0, first=True)
            with act.Fori(1, NB // 2 - 1) as m:
                for u in range(2):
                    block0_step(2 * m + u, 1 - u)
            block0_step(NB - 2, 1)
            block0_step(NB - 1, 0, last=True)
            softexp(NP - 1, 1)
            for u in range(2):
                softexp(NP + u, u)
            act.wait_ge(xt_lo, KD * NB)
            drain(0)

            def attention(b, last=False):
                with act.Fori(1, NP // 2) as h:
                    for u in range(2):
                        softexp(b * NP + 2 * h + u, u)
                if not last:
                    for u in range(2):
                        softexp((b + 1) * NP + u, u)
                drain(b)

            with act.Fori(1, NB - 1) as b:
                attention(b)
            attention(NB - 1, last=True)

            def copy_hT(b):
                act.wait_ge(ht_ok, b + 1)
                act.activation(xnTh[:, b * BLK:(b + 1) * BLK], sc16[:, b % 2, 0, :], ACT.Copy).then_inc(ht_hi, 1)
                act.activation(xnTl[:, b * BLK:(b + 1) * BLK], sc16[:, b % 2, 1, :], ACT.Copy).then_inc(ht_lo, 1)
            for b in range(NB - 1):
                copy_hT(b)
            act.wait_ge(lmax_ok, 1)
            act.activation(rt[:, 0, :], acc[:, 1, 0:E], ACT.Exp, bias=rc[:, 1:2]).then_inc(lexp_ok, 1)
            act.wait_ge(b1t_ok, 1)
            act.activation(b1cols[:, :], acc[:, 2, 0:E * FT], ACT.Copy).then_inc(b1c_ok, 1)
            act.activation(rc[:, 15:16], tcol[:, :], ACT.Gelu).then_inc(table_ok, 1)

            def w1_high(q):
                act.wait_ge(w1_in[q], 16)
                act.activation(w1h[:, q], w1f[:, q], ACT.Copy, scale=WSCALE).then_inc(w1_hi, 1)

            def w2_high(q):
                act.wait_ge(w2_sc, q + 1)
                act.activation(w2h[:, q], w2f[:, q], ACT.Copy).then_inc(w2_hi, 1)

            def gelus(q, u, n, fresh=False):
                act.wait_ge(up_ok, n + 1)
                if not fresh:
                    act.wait_ge(g_ok, n - 1)
                for s in range(2):
                    act.activation(ebuf[:, u, s * IB:(s + 1) * IB], sc[:, u, s, :], ACT.Gelu,
                                   bias=b1sel[:, 2 * q + s:2 * q + s + 1], scale=1.0 / WSCALE).then_inc(gelu_ok, 1)

            def ffn(b, last=False):
                for q in range(2, NQ):
                    gelus(q, q % 2, b * NQ + q)
                if not last:
                    for q in range(2):
                        gelus(q, q, (b + 1) * NQ + q)
                if last:
                    return
                act.wait_ge(down_ok, NQ * (b + 1))
                act.wait_ge(fin_ok, b)
                for t in range(TB):
                    act.activation(accs[:, t, 0:D], acc[:, t, 0:D], ACT.Copy, scale=1.0 / WSCALE).then_inc(y_out, 1)

            w1_high(0)
            act.wait_ge(ht_ok, NB)
            act.activation(xnTh[:, (NB - 1) * BLK:NB * BLK], acc16[:, 3, :], ACT.Copy).then_inc(ht_hi, 1)
            w2_high(0)
            w1_high(1)
            w2_high(1)
            act.wait_ge(b1sel_ok, TOP)
            act.wait_ge(table_ok, 1)
            for q in range(NQ):
                if q + 2 < NQ:
                    w1_high(q + 2)
                gelus(q, q % 2, q, fresh=(q < 2))
                if q + 2 < NQ:
                    w2_high(q + 2)
            for q in range(2):
                gelus(q, q, NQ + q)
            act.wait_ge(down_ok, NQ)
            for t in range(TB):
                act.activation(accs[:, t, 0:D], acc[:, t, 0:D], ACT.Copy, scale=1.0 / WSCALE).then_inc(y_out, 1)
            with act.Fori(1, NB - 1) as b:
                ffn(b)
            ffn(NB - 1, last=True)

        @block.vector
        def _(ve):
            ve.wait_ge(iota_ok, 1)
            ve.scalar_tensor_tensor(out=ltoe[:, 1, :], in0=ltoe[:, 0, :], scalar=-1.0, in1=ltoe[:, 0, :],
                                    op0=ALU.mult, op1=ALU.max).then_inc(lchain, 1)
            ve.wait_ge(lchain, 1)
            ve.tensor_scalar(ltoe[:, 2, :], ltoe[:, 1, :], EPS_W, None, ALU.add).then_inc(lchain, 1)
            ve.wait_ge(lchain, 2)
            ve.reciprocal(ltoe[:, 1, :], ltoe[:, 2, :]).then_inc(lchain, 1)
            ve.wait_ge(lchain, 3)
            ve.scalar_tensor_tensor(out=ltoe[:, 3, :], in0=ltoe[:, 0, :], scalar=0.0, in1=ltoe[:, 1, :],
                                    op0=ALU.not_equal, op1=ALU.mult).then_inc(ltoe_ok, 1)

            def norm_stats(src, n, u):
                if not isinstance(n, int) or n > 0:
                    ve.wait_ge(mv_ok, TB * n)
                ve.nop(nofuse=True)
                for t in range(TB):
                    ve.bn_stats(stats[:, u, t, :], src(t)).then_inc(st_ok, 1)
                ve.wait_ge(st_ok, TB * n + TB)
                ve.nop(nofuse=True)
                for t in range(TB):
                    ve.bn_aggr(mv[:, u, t, :], stats[:, u, t, :]).then_inc(mv_ok, 1)
                ve.wait_ge(mv_ok, TB * n + TB)

            def norm_var(n, u):
                ve.tensor_scalar(vtmp[:, u, :], mv[:, u, :, 1], EPS_LN, None, ALU.add).then_inc(var_ok, 1)

            def xtile(g):
                return lambda t: bass.AP(xres, (TB * g + t) * D, [[NT * D, P], [1, D]])

            def x_stats(g, u):
                if not isinstance(g, int) or g >= 2:
                    ve.wait_ge(xn_ok, g - 1)
                norm_stats(xtile(g), g, u)
                norm_var(g, u)

            def x_norm(g, u):
                ve.wait_ge(rstd_ok, g + 1)
                if not isinstance(g, int) or g >= 2:
                    ve.wait_ge(vl_ok, g - 1)
                for t in range(TB):
                    ins = ve.tensor_scalar(xn_f[:, u, t, :], xtile(g)(t), mv[:, u, t, 0:1],
                                           rstd[:, u, t:t + 1], ALU.subtract, ALU.mult)
                ins.then_inc(xn_ok, 1)

            def xt_split(g):
                for m in range(KD):
                    ve.wait_ge(xtf_ok, KD * g + m + 1)
                    src = xtf[:, m * IB:(m + 1) * IB]
                    ve.tensor_copy(tr(xtTh, g, m, 0, IB), src).then_inc(xt_hi, 1)
                    ve.wait_ge(xt_hi, KD * g + m + 1)
                    ve.tensor_tensor(tr(xtTl, g, m, 0, IB), src, tr(xtTh, g, m, 0, IB), ALU.subtract).then_inc(xt_lo, 1)

            def weigh(b, jp, u):
                ve.wait_ge(scores_ok, b * NP + jp + 1)
                ve.tensor_tensor(zbuf[:, u].rearrange("p (s c) -> p s c", s=2), sc[:, u], lwpair(b, jp),
                                 ALU.mult).then_inc(z_ok, 1)

            def split(n, u, fresh=False):
                ve.wait_ge(exp_ok, n + 1)
                if not fresh:
                    ve.wait_ge(pv_ok, n - 1)
                ve.tensor_copy(ph[:, u], ebuf[:, u]).then_inc(phi_ok, 1)
                ve.wait_ge(phi_ok, n + 1)
                ve.tensor_tensor(pl[:, u], ebuf[:, u], ph[:, u], ALU.subtract).then_inc(p_ok, 1)

            accd = accs[:, :, 0:D]

            def epi_diag(b):
                ve.wait_ge(acc_out, TB * (b + 1))
                ve.tensor_scalar(den[:, :], accs[:, :, D], -1.0, EPS_W, ALU.add, ALU.add).then_inc(ec, 1)
                ve.wait_ge(xdiag_ok, b + 1)
                ve.tensor_tensor(accd, accd, xdiag, ALU.subtract).then_inc(ec, 1)

            def epi_rden(b):
                ve.wait_ge(ec, EC * b + 2)
                ve.reciprocal(rden[:, :], den[:, :]).then_inc(ec, 1)
                ve.wait_ge(ec, EC * b + 3)
                ve.tensor_tensor(rden2[:, :], rden[:, :], rden[:, :], ALU.mult).then_inc(ec, 1)

            def epi_att_stats(b):
                norm_stats(lambda t: accs[:, t, 0:D], NB + 2 * b, 0)

            def epi_att_var(b):
                ve.wait_ge(ec, EC * b + 4)
                ve.tensor_tensor(vsc[:, :], mv[:, 0, :, 1], rden2[:, :], ALU.mult).then_inc(ec, 1)
                ve.wait_ge(ec, EC * b + 5)
                ve.tensor_scalar(vtmp[:, 0, :], vsc[:, :], EPS_LN, None, ALU.add).then_inc(var_ok, 1)

            def epi_x1(b):
                ve.wait_ge(rstd_ok, NB + 2 * b + 1)
                ve.tensor_tensor(kfac[:, :], rstd[:, 0, :], rden[:, :], ALU.mult).then_inc(ec, 1)
                ve.wait_ge(ec, EC * b + 6)
                for t in range(TB):
                    ve.scalar_tensor_tensor(out=xtile(b)(t), in0=accs[:, t, 0:D], scalar=kfac[:, t:t + 1],
                                            in1=xtile(b)(t), op0=ALU.mult, op1=ALU.add).then_inc(ec, 1)
                ve.wait_ge(x1_kept, b + 1)
                ve.tensor_tensor(mk[:, :], mv[:, 0, :, 0], kfac[:, :], ALU.mult).then_inc(ec, 1)

            def epi_x1_stats(b):
                ve.wait_ge(ec, EC * b + 7 + TB)
                norm_stats(xtile(b), NB + 2 * b + 1, 1)
                norm_var(NB + 2 * b + 1, 1)

            def epi_h(b):
                ve.wait_ge(rstd_ok, NB + 2 * b + 2)
                for t in range(TB):
                    ve.tensor_scalar(accs[:, t, 0:D], xtile(b)(t),
                                     mv[:, 1, t, 0:1], rstd[:, 1, t:t + 1], ALU.subtract, ALU.mult).then_inc(ec, 1)

            def epi_h_sum(b):
                ve.wait_ge(ec, EC * b + 7 + 2 * TB)
                ve.tensor_reduce(htot[:, :], accs[:, :, 0:D].rearrange("p t d -> p d t"), AX_X, ALU.add).then_inc(ec, 1)
                ve.wait_ge(ec, EC * b + 8 + 2 * TB)
                ve.tensor_tensor(hsum[:, :], hsum[:, :], htot[:, :], ALU.add).then_inc(hs_ok, 1)

            def epi_h_hi(b):
                hh = bass.AP(xtTh, b * BLK, [[NB * BLK, P], [D, TB], [1, D]])
                ve.tensor_copy(hh, accd).then_inc(ec, 1)

            def epi_h_lo(b):
                ve.wait_ge(ec, EC * (b + 1))
                hh = bass.AP(xtTh, b * BLK, [[NB * BLK, P], [D, TB], [1, D]])
                hl = bass.AP(xtTl, b * BLK, [[NB * BLK, P], [D, TB], [1, D]])
                ve.tensor_tensor(hl, accd, hh, ALU.subtract).then_inc(epi_ok, 1)

            ve.wait_ge(x_in[0], 16)
            x_stats(0, 0)
            ve.wait_ge(w_in, 16)
            ve.wait_ge(w_hi, 1)
            ve.scalar_tensor_tensor(out=Wl[:, :, :], in0=Wf[:, :, :], scalar=WSCALE, in1=Wh[:, :, :],
                                    op0=ALU.mult, op1=ALU.subtract).then_inc(w_lo, 1)
            x_norm(0, 0)
            ve.wait_ge(xn_ok, 1)
            ve.tensor_copy(vblock(0, 0, D), xn_f[:, 0]).then_inc(vh_ok, 1)
            ve.wait_ge(vh_ok, 1)
            ve.tensor_tensor(vblock(0, VLO, D), xn_f[:, 0], vblock(0, 0, D), ALU.subtract).then_inc(vl_ok, 1)
            ve.wait_ge(x_in[1], 16)
            x_stats(1, 1)
            xt_split(0)
            x_norm(1, 1)
            ve.wait_ge(vh_ok, 2)
            ve.tensor_tensor(vblock(1, VLO, D), xn_f[:, 1], vblock(1, 0, D), ALU.subtract).then_inc(vl_ok, 1)
            ve.wait_ge(consts, 7)
            ve.wait_ge(lw_in[0], 16)
            weigh(0, 0, 0)
            weigh(0, 1, 1)
            ve.wait_ge(x_in[2], 16)
            x_stats(2, 0)
            split(0, 0, fresh=True)

            def block0_step(g, v, left=2):
                if left >= 1:
                    x_norm(g + 1, v)
                weigh(0, 2 * g, 0)
                split(2 * g - 1, 1, fresh=(isinstance(g, int) and g == 1))
                xt_split(g)
                weigh(0, 2 * g + 1, 1)
                if left >= 2:
                    x_stats(g + 2, 1 - v)
                split(2 * g, 0)
            ve.wait_ge(x_in[3], 16)
            block0_step(1, 0)
            ve.wait_ge(xrest_in, 16 * (NB - 4))
            ve.wait_ge(lw_in[1], 16)
            with ve.Fori(1, NB // 2 - 1) as m:
                for u in range(2):
                    block0_step(2 * m + u, 1 - u)
            block0_step(NB - 2, 1, left=1)
            block0_step(NB - 1, 0, left=0)
            ve.wait_ge(lw_in[2], 16)
            for jp in range(2):
                weigh(1, jp, jp)
                split(NP - 1 + jp, 1 - jp)

            def attention(b, last=False):
                for jp in range(2, 10):
                    weigh(b, jp, jp % 2)
                    split(b * NP + jp - 1, (jp - 1) % 2)
                    if jp == 2:
                        epi_diag(b - 1)
                    if jp == 3:
                        epi_rden(b - 1)
                    if jp == 4:
                        epi_att_stats(b - 1)
                        epi_att_var(b - 1)
                    if jp == 5:
                        epi_x1(b - 1)
                    if jp == 6:
                        epi_x1_stats(b - 1)
                    if jp == 7:
                        epi_h(b - 1)
                    if jp == 8:
                        epi_h_sum(b - 1)
                        epi_h_hi(b - 1)
                    if jp == 9:
                        epi_h_lo(b - 1)
                with ve.Fori(5, NP // 2) as h:
                    for u in range(2):
                        weigh(b, 2 * h + u, u)
                        split(b * NP + 2 * h + u - 1, 1 - u)
                for jp in range(2):
                    if not last:
                        weigh(b + 1, jp, jp)
                    if jp == 0 or not last:
                        split(b * NP + NP + jp - 1, 1 - jp)

            with ve.Fori(1, NB - 1) as b:
                attention(b)
            attention(NB - 1, last=True)

            def part_stats(src, n, u, ts):
                for t in range(ts.start, ts.stop):
                    ve.bn_stats(stats[:, u, t, :], src(t)).then_inc(st_ok, 1)
                ve.wait_ge(st_ok, TB * n + ts.stop)
                for t in range(ts.start, ts.stop):
                    ve.bn_aggr(mv[:, u, t, :], stats[:, u, t, :]).then_inc(mv_ok, 1)
                ve.wait_ge(mv_ok, TB * n + ts.stop)

            steps = [0]

            def did(ins):
                ins.then_inc(lastb, 1)
                steps[0] += 1
                return steps[0]
            b = NB - 1
            x2 = [bass.AP(xres, (b * TB + t) * D, [[NT * D, P], [1, D]]) for t in range(TB)]
            diag = []
            ve.wait_ge(xdiag_ok, NB)
            for ts in halves:
                ve.wait_ge(acc_out, TB * b + ts.stop)
                den_made = did(ve.tensor_scalar(den[:, ts], accs[:, ts, D], -1.0, EPS_W, ALU.add, ALU.add))
                diag.append(did(ve.tensor_tensor(accs[:, ts, 0:D], accs[:, ts, 0:D], xdiag[:, ts], ALU.subtract)))
                ve.wait_ge(lastb, den_made)
                ve.reciprocal(rden[:, ts], den[:, ts]).then_inc(lastb, 1)
                steps[0] += 1
            for i, ts in enumerate(halves):
                ve.wait_ge(lastb, diag[i] + 1)
                squared = did(ve.tensor_tensor(rden2[:, ts], rden[:, ts], rden[:, ts], ALU.mult))
                part_stats(lambda t: accs[:, t, 0:D], 3 * NB - 2, 0, ts)
                ve.wait_ge(lastb, squared)
                scaled = did(ve.tensor_tensor(vsc[:, ts], mv[:, 0, ts, 1], rden2[:, ts], ALU.mult))
                ve.wait_ge(lastb, scaled)
                ve.tensor_scalar(vtmp[:, 0, ts], vsc[:, ts], EPS_LN, None, ALU.add).then_inc(var_ok, 1)
            x1_made = []
            ve.wait_ge(x1_kept, b + 1)
            for i, ts in enumerate(halves):
                ve.wait_ge(rstd_ok, 3 * NB - 2 + i + 1)
                kfac_made = did(ve.tensor_tensor(kfac[:, ts], rstd[:, 0, ts], rden[:, ts], ALU.mult))
                ve.wait_ge(lastb, kfac_made)
                did(ve.tensor_tensor(mk[:, ts], mv[:, 0, ts, 0], kfac[:, ts], ALU.mult))
                for t in range(ts.start, ts.stop):
                    made = did(ve.scalar_tensor_tensor(out=x2[t], in0=accs[:, t, 0:D], scalar=kfac[:, t:t + 1],
                                                       in1=x2[t], op0=ALU.mult, op1=ALU.add))
                x1_made.append(made)
            for i, ts in enumerate(halves):
                ve.wait_ge(lastb, x1_made[i])
                part_stats(lambda t: x2[t], 3 * NB - 1, 1, ts)
                ve.tensor_scalar(vtmp[:, 1, ts], mv[:, 1, ts, 1], EPS_LN, None, ALU.add).then_inc(var_ok, 1)
            for i, ts in enumerate(halves):
                ve.wait_ge(rstd_ok, 3 * NB + i + 1)
                for t in range(ts.start, ts.stop):
                    h_made = did(ve.tensor_scalar(accs[:, t, 0:D], x2[t], mv[:, 1, t, 0:1], rstd[:, 1, t:t + 1],
                                                  ALU.subtract, ALU.mult))
            ve.wait_ge(lastb, h_made)
            summed = did(ve.tensor_reduce(htot[:, :], accs[:, :, 0:D].rearrange("p t d -> p d t"), AX_X, ALU.add))
            ve.wait_ge(lastb, summed)
            ve.tensor_tensor(hsum[:, :], hsum[:, :], htot[:, :], ALU.add).then_inc(hs_ok, 1)
            hh = bass.AP(xtTh, b * BLK, [[NB * BLK, P], [D, TB], [1, D]])
            hl = bass.AP(xtTl, b * BLK, [[NB * BLK, P], [D, TB], [1, D]])
            h_hi = did(ve.tensor_copy(hh, accd))

            links = [0]

            def link(ins):
                links[0] += 1
                ins.then_inc(rchain, 1)
                ve.wait_ge(rchain, links[0])
            LMAX, NLMAX, ESUM, ERCP, P1, R1, P2, R2, PS, PR, C1, C2 = (rc[:, i:i + 1] for i in range(12))
            EXPS, PROBS, CAND1, ONE1, REST, CAND2, ONE2, COMB1 = (rt[:, i, :] for i in range(8))
            ve.wait_ge(hmean_ok, 1)
            link(ve.tensor_copy(meanT[:, :], acc[:, 0, 0:KD]))
            for k in range(KD):
                ve.tensor_scalar(meanB[:, k, :], ones[:, :], meanT[:, k:k + 1], None, ALU.mult).then_inc(meanT_ok, 1)
            ve.wait_ge(logit_ok, 1)
            link(ve.tensor_reduce(LMAX, acc[:, 1, 0:E], AX_X, ALU.max))
            ve.tensor_scalar(NLMAX, LMAX, -1.0, None, ALU.mult).then_inc(lmax_ok, 1)
            ve.wait_ge(lexp_ok, 1)
            link(ve.tensor_reduce(ESUM, EXPS, AX_X, ALU.add))
            link(ve.reciprocal(ERCP, ESUM))
            link(ve.tensor_scalar(PROBS, EXPS, ERCP, None, ALU.mult))
            link(ve.tensor_reduce(P1, PROBS, AX_X, ALU.max))
            link(ve.scalar_tensor_tensor(out=CAND1, in0=PROBS, scalar=P1, in1=rev[:, :],
                                         op0=ALU.is_equal, op1=ALU.mult))
            link(ve.tensor_reduce(R1, CAND1, AX_X, ALU.max))
            ve.tensor_scalar(eidx[:, 0:1], R1, -1.0, float(E), ALU.mult, ALU.add).then_inc(route_ok, 1)
            link(ve.tensor_scalar(ONE1, rev[:, :], R1, None, ALU.is_equal))
            link(ve.scalar_tensor_tensor(out=REST, in0=ONE1, scalar=-2.0, in1=PROBS, op0=ALU.mult, op1=ALU.add))
            link(ve.tensor_reduce(P2, REST, AX_X, ALU.max))
            link(ve.scalar_tensor_tensor(out=CAND2, in0=REST, scalar=P2, in1=rev[:, :],
                                         op0=ALU.is_equal, op1=ALU.mult))
            link(ve.tensor_reduce(R2, CAND2, AX_X, ALU.max))
            ve.tensor_scalar(eidx[:, 1:2], R2, -1.0, float(E), ALU.mult, ALU.add).then_inc(route_ok, 1)
            ve.wait_ge(lastb, h_hi)
            ve.tensor_tensor(hl, accd, hh, ALU.subtract).then_inc(epi_ok, 1)
            link(ve.tensor_scalar(ONE2, rev[:, :], R2, None, ALU.is_equal))
            link(ve.tensor_tensor(PS, P1, P2, ALU.add))
            link(ve.reciprocal(PR, PS))
            link(ve.tensor_tensor(C1, P1, PR, ALU.mult))
            link(ve.tensor_tensor(C2, P2, PR, ALU.mult))
            link(ve.tensor_scalar(COMB1, ONE1, C1, None, ALU.mult))
            link(ve.scalar_tensor_tensor(out=comb[:, :], in0=ONE2, scalar=C2, in1=COMB1, op0=ALU.mult, op1=ALU.add))
            ve.wait_ge(b1c_ok, 1)
            for i, one in enumerate((ONE1, ONE2)):
                link(ve.tensor_tensor(bprod[:, i], b1cols[:, :].rearrange("p (e t) -> p t e", e=E),
                                      one.unsqueeze(1).broadcast_to([P, FT, E]), ALU.mult))
                ve.tensor_reduce(b1sel[:, i * FT:(i + 1) * FT], bprod[:, i], AX_X, ALU.add).then_inc(b1sel_ok, 1)

            def w2_scale(q):
                ve.wait_ge(w2_in[q], 16)
                ve.tensor_scalar(w2f[:, q], w2f[:, q], (C1, C2)[q // FP], WSCALE, ALU.mult, ALU.mult).then_inc(w2_sc, 1)

            def w1_split(q):
                ve.wait_ge(w1_hi, q + 1)
                ve.scalar_tensor_tensor(out=w1l[:, q], in0=w1f[:, q], scalar=WSCALE, in1=w1h[:, q],
                                        op0=ALU.mult, op1=ALU.subtract).then_inc(w1_lo, 1)

            def w2_split(q):
                ve.wait_ge(w2_hi, q + 1)
                ve.tensor_tensor(w2l[:, q], w2f[:, q], w2h[:, q], ALU.subtract).then_inc(w2_lo, 1)

            def gsplit(n, u, fresh=False):
                ve.wait_ge(gelu_ok, 2 * n + 2)
                if not fresh:
                    ve.wait_ge(down_ok, n - 1)
                ve.tensor_copy(ph[:, u], ebuf[:, u]).then_inc(ghi_ok, 1)
                ve.wait_ge(ghi_ok, n + 1)
                ve.tensor_tensor(pl[:, u], ebuf[:, u], ph[:, u], ALU.subtract).then_inc(g_ok, 1)

            def fin_bias(b):
                ve.wait_ge(y_out, TB * (b + 1))
                ve.tensor_tensor(accd, accd, b2c[:, :].unsqueeze(1).broadcast_to([P, TB, D]), ALU.add).then_inc(fc, 1)

            def fin_stats(b):
                ve.wait_ge(fc, (TB + 1) * b + 1)
                norm_stats(lambda t: accs[:, t, 0:D], 3 * NB + b, 0)
                norm_var(3 * NB + b, 0)

            def fin_norm(b):
                ve.wait_ge(rstd_ok, PF + b + 1)
                for t in range(TB):
                    ve.tensor_scalar(accs[:, t, 0:D], accs[:, t, 0:D], mv[:, 0, t, 0:1], rstd[:, 0, t:t + 1],
                                     ALU.subtract, ALU.mult).then_inc(fc, 1)

            def fin_add(b):
                ve.wait_ge(fc, (TB + 1) * (b + 1))
                x2 = bass.AP(xres, b * TB * D, [[NT * D, P], [D, TB], [1, D]])
                ve.tensor_tensor(x2, x2, accd, ALU.add).then_inc(fin_ok, 1)

            w1_split(0)
            ve.wait_ge(ht_ok, NB)
            ve.tensor_copy(xnTl[:, (NB - 1) * BLK:NB * BLK], acc16[:, 0, :]).then_inc(ht_lo, 1)
            w2_scale(0)
            w1_split(1)
            w2_scale(1)
            w2_split(0)
            for q in range(NQ):
                if q + 2 < NQ:
                    w1_split(q + 2)
                    w2_scale(q + 2)
                gsplit(q, q % 2, fresh=(q < 2))
                if q + 1 < NQ:
                    w2_split(q + 1)
                if q == 3:
                    ve.wait_ge(b2_in, 16)
                    link(ve.tensor_scalar(b2c[:, :], b2all[:, 0, :], comb[:, 0:1], None, ALU.mult))
                if q >= 4 and q < 4 + (E - 1 + 1) // 2:
                    for e in range(1 + 2 * (q - 4), min(3 + 2 * (q - 4), E)):
                        link(ve.scalar_tensor_tensor(out=b2c[:, :], in0=b2all[:, e, :], scalar=comb[:, e:e + 1],
                                                     in1=b2c[:, :], op0=ALU.mult, op1=ALU.add))

            def ffn(b):
                for q in range(NQ):
                    gsplit(b * NQ + q, q % 2)
                    if q == 2:
                        fin_bias(b - 1)
                    if q == 3:
                        fin_stats(b - 1)
                    if q == 4:
                        fin_norm(b - 1)
                    if q == 5:
                        fin_add(b - 1)
            ve.wait_ge(x1_kept, NB + 1)
            with ve.Fori(1, NB) as b:
                ffn(b)

            last = 4 * NB - 1
            ve.wait_ge(fin_ok, NB - 1)
            for i, ts in enumerate(halves):
                for t in range(ts.start, ts.stop):
                    ve.wait_ge(last_down, t + 1)
                    ve.scalar_tensor_tensor(out=accs[:, t, 0:D], in0=acc[:, t, 0:D], scalar=1.0 / WSCALE, in1=b2c[:, :],
                                            op0=ALU.mult, op1=ALU.add).then_inc(tail, 1)
                ve.wait_ge(tail, ts.stop)
                part_stats(lambda t: accs[:, t, 0:D], last, 0, ts)
                ve.tensor_scalar(vtmp[:, 0, ts], mv[:, 0, ts, 1], EPS_LN, None, ALU.add).then_inc(var_ok, 1)
            for i, ts in enumerate(halves):
                ve.wait_ge(rstd_ok, PF + NB + i)
                for t in range(ts.start, ts.stop):
                    ve.tensor_scalar(accs[:, t, 0:D], accs[:, t, 0:D], mv[:, 0, t, 0:1], rstd[:, 0, t:t + 1],
                                     ALU.subtract, ALU.mult).then_inc(tail, 1)
                ve.wait_ge(tail, TB + ts.stop)
                x1 = xres[:, NT - TB + ts.start:NT - TB + ts.stop, :]
                ve.tensor_tensor(x1, x1, accs[:, ts, 0:D], ALU.add).then_inc(fin_ok, 1)


_INS = ['L0_attn_x', 'L0_attn_W', 'L0_attn_b', 'L0_ffn_gate_w', 'L0_ffn_w1', 'L0_ffn_b1', 'L0_ffn_w2', 'L0_ffn_b2']
_OUTS = [((1, 4096, 256), 'float32')]


def kernel(**inputs):
    import numpy as _np
    import concourse.bacc as _bacc
    from concourse import mybir as _mybir
    from concourse.bass_utils import run_bass_kernel_spmd as _run

    nc = _bacc.Bacc("TRN2", target_bir_lowering=False, num_devices=1)
    arrays, args = {}, []
    for name in _INS:
        a = _np.ascontiguousarray(inputs[name])
        arrays[f"in_{name}_dram"] = a
        args.append(nc.dram_tensor(f"in_{name}_dram", a.shape, _mybir.dt.from_np(a.dtype), kind="ExternalInput").ap())
    for i, (shape, dtype) in enumerate(_OUTS):
        dt = _mybir.dt.from_np(_np.dtype(dtype))
        args.append(nc.dram_tensor(f"out_{i}_dram", shape, dt, kind="ExternalOutput").ap())
    program(nc, *args)
    r = _run(nc, [arrays], core_ids=[0])
    return r.results[0]["out_0_dram"]
```
